# Optimizing a Trainium2 kernel written in Bass

```python
import numpy as np
import jax
import jax.numpy as jnp

def _softmax(x, axis=-1):
    return jax.nn.softmax(x, axis=axis)

def _gelu(x):
    return jax.nn.gelu(x, approximate=True)

def _silu(x):
    return jax.nn.silu(x)

def _sigmoid(x):
    return jax.nn.sigmoid(x)

def _layernorm(x, axis=-1, eps=1e-05):
    m = jnp.mean(x, axis=axis, keepdims=True)
    v = jnp.var(x, axis=axis, keepdims=True)
    return (x - m) / jnp.sqrt(v + eps)

def _scatter_add(tgt, idx, src, axis=0):
    return tgt.at[idx].add(src)

def _segment_sum(src, seg, n):
    return jax.ops.segment_sum(src, seg, n)
kernel_name = 'mk_xattn_ffn_d1_seqx_r4_57a114'

def setup_inputs(seed: int=0):
    np.random.seed(seed)
    _w = jnp.asarray

    def _rec_inputs():
        import jax
        import jax.numpy as jnp
        _rk = jax.random.key(seed)
        x = -0.000125 + 0.9999 * jax.random.normal(jax.random.fold_in(_rk, 1), (2, 1024, 256), jnp.float32)
        _lenS = 1024 - jax.random.randint(jax.random.fold_in(_rk, 7), (2,), 0, max(1, 1024 // 4) + 1, jnp.int32)
        _lenS2 = 77 - jax.random.randint(jax.random.fold_in(_rk, 8), (2,), 0, max(1, 77 // 4) + 1, jnp.int32)
        _ctx_1024P = jax.random.normal(jax.random.fold_in(_rk, 11), (2, 16, 256), jnp.float32)
        _ctx_1024c = jax.random.dirichlet(jax.random.fold_in(_rk, 511), 0.3 * jnp.ones((16,), jnp.float32), (2, 77))
        _ctx_1024t = jnp.einsum('bsk,bkd->bsd', _ctx_1024c, _ctx_1024P)
        _ctx_1024t = _ctx_1024t * jax.lax.rsqrt(jnp.mean(jnp.square(_ctx_1024t)) + 1e-12) * 0.953939
        ctx_1024 = -1.52775e-05 + 0.999936 * (_ctx_1024t + 0.3 * jax.random.normal(jax.random.fold_in(_rk, 611), (2, 77, 256), jnp.float32))
        _validS = jnp.arange(1024)[None, :] < _lenS[:, None]
        _validS2 = jnp.arange(77)[None, :] < _lenS2[:, None]
        _causal = jnp.tril(jnp.ones((1024, 1024), dtype=bool))
        mask_BxS2_if1 = jnp.where(jnp.ones((2, 77), dtype=bool), 1, 0).astype(jnp.int32)
        return (x, ctx_1024, mask_BxS2_if1)
    x, ctx_1024, mask_BxS2_if1 = _rec_inputs()

    def _L0_xattn_setup():
        import jax, jax.numpy as jnp
        import numpy as np
        NEG = -10000.0
        key = jax.random.key(seed)
        k1, k2, k3 = jax.random.split(key, 3)
        B, L, D, H = (16, 512, 256, 256)
        x1 = jax.random.normal(k1, (B, L, D), dtype=jnp.float32)
        x2 = jax.random.normal(k2, (B, L, D), dtype=jnp.float32)
        x2_mask = jnp.ones((B, L), dtype=jnp.int64)
        W = jax.random.normal(k3, (H, D), dtype=jnp.float32) * (1.0 / np.sqrt(D))
        diagonal = jnp.ones((H,), dtype=jnp.float32)
        return {'x1': x1, 'x2': x2, 'x2_mask': x2_mask, 'W': W, 'diagonal': diagonal}
    _L0_xattn_all = _L0_xattn_setup()
    _L0_xattn_in = {k: v for k, v in _L0_xattn_all.items() if k in ('W', 'diagonal')}
    del _L0_xattn_all

    def _L0_ffn_setup():
        import jax, jax.numpy as jnp
        import numpy as np
        D = 256
        H = 4
        HD = D // H
        E = 8
        FF = 1024
        CAP_FACTOR = 1.0

        def _ln(x, g, b, eps=1e-05):
            mu = jnp.mean(x, -1, keepdims=True)
            v = jnp.mean((x - mu) ** 2, -1, keepdims=True)
            return (x - mu) * jax.lax.rsqrt(v + eps) * g + b

        def _mha(x, w, b, ow, ob):
            L, N, _ = x.shape
            qkv = x @ w.T + b
            q, k, v = jnp.split(qkv, 3, axis=-1)
            rh = lambda t: t.reshape(L, N, H, HD).transpose(1, 2, 0, 3)
            q, k, v = (rh(q), rh(k), rh(v))
            scores = jnp.einsum('nhld,nhmd->nhlm', q, k) / np.float32(np.sqrt(HD))
            attn = jax.nn.softmax(scores, axis=-1)
            o = jnp.einsum('nhlm,nhmd->nhld', attn, v).transpose(2, 0, 1, 3).reshape(L, N, D)
            return o @ ow.T + ob

        def _moe(x, wg, w1, b1, w2, b2):
            L, N, _ = x.shape
            S = L * N
            cap = int(CAP_FACTOR * S) // E
            xf = x.reshape(S, D)
            gates = jax.nn.softmax(xf @ wg, axis=-1)
            idx = jnp.argmax(gates, axis=-1)
            mask1 = jax.nn.one_hot(idx, E, dtype=x.dtype)
            loc = jnp.sum((jnp.cumsum(mask1, 0) - 1.0) * mask1, -1).astype(jnp.int32)
            keep = loc < cap
            gate_val = jnp.take_along_axis(gates, idx[:, None], -1)[:, 0]
            slot = jnp.where(keep, idx.astype(jnp.int32) * cap + loc, E * cap)
            disp = jnp.zeros((E * cap, D), x.dtype).at[slot].set(xf, mode='drop')
            disp = disp.reshape(E, cap, D)
            h = jnp.einsum('ecd,edf->ecf', disp, w1) + b1[:, None, :]
            y = (jnp.einsum('ecf,efd->ecd', h, w2) + b2[:, None, :]).reshape(E * cap, D)
            out = jnp.where(keep[:, None], gate_val[:, None] * y[jnp.minimum(slot, E * cap - 1)], 0.0)
            return out.reshape(L, N, D)
        key = jax.random.key(seed)
        ks = jax.random.split(key, 8)
        L, N = (256, 16)
        s = 0.02
        return {'x': jax.random.normal(ks[0], (L, N, D), jnp.float32), 'in_proj_w': jax.random.normal(ks[1], (3 * D, D), jnp.float32) * s, 'in_proj_b': jnp.zeros((3 * D,), jnp.float32), 'out_proj_w': jax.random.normal(ks[2], (D, D), jnp.float32) * s, 'out_proj_b': jnp.zeros((D,), jnp.float32), 'ln1_g': jnp.ones((D,), jnp.float32), 'ln1_b': jnp.zeros((D,), jnp.float32), 'ln2_g': jnp.ones((D,), jnp.float32), 'ln2_b': jnp.zeros((D,), jnp.float32), 'wg': jax.random.normal(ks[3], (D, E), jnp.float32) * s, 'w1': jax.random.normal(ks[4], (E, D, FF), jnp.float32) * s, 'b1': jnp.zeros((E, FF), jnp.float32), 'w2': jax.random.normal(ks[5], (E, FF, D), jnp.float32) * s, 'b2': jnp.zeros((E, D), jnp.float32)}
    _L0_ffn_all = _L0_ffn_setup()
    _L0_ffn_in = {k: v for k, v in _L0_ffn_all.items() if k in ('in_proj_w', 'in_proj_b', 'out_proj_w', 'out_proj_b', 'ln1_g', 'ln1_b', 'ln2_g', 'ln2_b', 'wg', 'w1', 'b1', 'w2', 'b2')}
    del _L0_ffn_all
    return {'x': x, 'ctx_1024': ctx_1024, 'mask_BxS2_if1': mask_BxS2_if1, 'L0_xattn_W': _L0_xattn_in['W'], 'L0_xattn_diagonal': _L0_xattn_in['diagonal'], 'L0_ffn_in_proj_w': _L0_ffn_in['in_proj_w'], 'L0_ffn_in_proj_b': _L0_ffn_in['in_proj_b'], 'L0_ffn_out_proj_w': _L0_ffn_in['out_proj_w'], 'L0_ffn_out_proj_b': _L0_ffn_in['out_proj_b'], 'L0_ffn_ln1_g': _L0_ffn_in['ln1_g'], 'L0_ffn_ln1_b': _L0_ffn_in['ln1_b'], 'L0_ffn_ln2_g': _L0_ffn_in['ln2_g'], 'L0_ffn_ln2_b': _L0_ffn_in['ln2_b'], 'L0_ffn_wg': _L0_ffn_in['wg'], 'L0_ffn_w1': _L0_ffn_in['w1'], 'L0_ffn_b1': _L0_ffn_in['b1'], 'L0_ffn_w2': _L0_ffn_in['w2'], 'L0_ffn_b2': _L0_ffn_in['b2']}

def reference(x, ctx_1024, mask_BxS2_if1, L0_xattn_W, L0_xattn_diagonal, L0_ffn_in_proj_w, L0_ffn_in_proj_b, L0_ffn_out_proj_w, L0_ffn_out_proj_b, L0_ffn_ln1_g, L0_ffn_ln1_b, L0_ffn_ln2_g, L0_ffn_ln2_b, L0_ffn_wg, L0_ffn_w1, L0_ffn_b1, L0_ffn_w2, L0_ffn_b2):
    import jax
    import jax.numpy as jnp

    def _L0_xattn_ref(x1, x2, x2_mask, W, diagonal):
        import jax, jax.numpy as jnp
        import numpy as np
        NEG = -10000.0
        x1_rep = jax.nn.relu(jnp.einsum('bld,hd->blh', x1, W))
        x2_rep = jax.nn.relu(jnp.einsum('bld,hd->blh', x2, W))
        scores = jnp.einsum('bih,bjh->bij', x1_rep * diagonal, x2_rep)
        m = (1.0 - x2_mask.astype(scores.dtype)) * NEG
        alpha = jax.nn.softmax(scores + m[:, None, :], axis=-1)
        return jnp.einsum('bij,bjd->bid', alpha, x2)

    def _L0_ffn_ref(x, in_proj_w, in_proj_b, out_proj_w, out_proj_b, ln1_g, ln1_b, ln2_g, ln2_b, wg, w1, b1, w2, b2):
        import jax, jax.numpy as jnp
        import numpy as np
        D = 256
        H = 4
        HD = D // H
        E = 8
        FF = 1024
        CAP_FACTOR = 1.0

        def _ln(x, g, b, eps=1e-05):
            mu = jnp.mean(x, -1, keepdims=True)
            v = jnp.mean((x - mu) ** 2, -1, keepdims=True)
            return (x - mu) * jax.lax.rsqrt(v + eps) * g + b

        def _mha(x, w, b, ow, ob):
            L, N, _ = x.shape
            qkv = x @ w.T + b
            q, k, v = jnp.split(qkv, 3, axis=-1)
            rh = lambda t: t.reshape(L, N, H, HD).transpose(1, 2, 0, 3)
            q, k, v = (rh(q), rh(k), rh(v))
            scores = jnp.einsum('nhld,nhmd->nhlm', q, k) / np.float32(np.sqrt(HD))
            attn = jax.nn.softmax(scores, axis=-1)
            o = jnp.einsum('nhlm,nhmd->nhld', attn, v).transpose(2, 0, 1, 3).reshape(L, N, D)
            return o @ ow.T + ob

        def _moe(x, wg, w1, b1, w2, b2):
            L, N, _ = x.shape
            S = L * N
            cap = int(CAP_FACTOR * S) // E
            xf = x.reshape(S, D)
            gates = jax.nn.softmax(xf @ wg, axis=-1)
            idx = jnp.argmax(gates, axis=-1)
            mask1 = jax.nn.one_hot(idx, E, dtype=x.dtype)
            loc = jnp.sum((jnp.cumsum(mask1, 0) - 1.0) * mask1, -1).astype(jnp.int32)
            keep = loc < cap
            gate_val = jnp.take_along_axis(gates, idx[:, None], -1)[:, 0]
            slot = jnp.where(keep, idx.astype(jnp.int32) * cap + loc, E * cap)
            disp = jnp.zeros((E * cap, D), x.dtype).at[slot].set(xf, mode='drop')
            disp = disp.reshape(E, cap, D)
            h = jnp.einsum('ecd,edf->ecf', disp, w1) + b1[:, None, :]
            y = (jnp.einsum('ecf,efd->ecd', h, w2) + b2[:, None, :]).reshape(E * cap, D)
            out = jnp.where(keep[:, None], gate_val[:, None] * y[jnp.minimum(slot, E * cap - 1)], 0.0)
            return out.reshape(L, N, D)
        y1 = _ln(x + _mha(x, in_proj_w, in_proj_b, out_proj_w, out_proj_b), ln1_g, ln1_b)
        y2 = _ln(y1 + _moe(y1, wg, w1, b1, w2, b2), ln2_g, ln2_b)
        return y2
    x = x + _L0_xattn_ref(_layernorm(x, axis=-1), ctx_1024, mask_BxS2_if1, L0_xattn_W, L0_xattn_diagonal)
    x = x + _L0_ffn_ref(_layernorm(x, axis=-1), L0_ffn_in_proj_w, L0_ffn_in_proj_b, L0_ffn_out_proj_w, L0_ffn_out_proj_b, L0_ffn_ln1_g, L0_ffn_ln1_b, L0_ffn_ln2_g, L0_ffn_ln2_b, L0_ffn_wg, L0_ffn_w1, L0_ffn_b1, L0_ffn_w2, L0_ffn_b2)
    return x

_drawn_inputs = setup_inputs


def setup_inputs(seed=0):
    import zlib

    import numpy as np

    out = dict(_drawn_inputs(seed))
    spreads = {'L0_xattn_diagonal': (1.0, 0.2),
     'L0_ffn_in_proj_b': (0.0, 0.665),
     'L0_ffn_out_proj_b': (0.0, 0.1),
     'L0_ffn_ln1_g': (1.0, 0.2),
     'L0_ffn_ln1_b': (0.0, 0.1),
     'L0_ffn_ln2_g': (1.0, 0.2),
     'L0_ffn_ln2_b': (0.0, 0.1),
     'L0_ffn_b1': (0.0, 0.8),
     'L0_ffn_b2': (0.0, 0.8)}
    factors = {'L0_ffn_wg': 4.087, 'L0_ffn_w1': 4.37, 'L0_ffn_w2': 4.094}
    for name, (base, spread) in spreads.items():
        noise = np.random.default_rng([zlib.crc32(name.encode()), seed]).standard_normal(out[name].shape)
        drawn = base * np.exp(spread * noise) if base else spread * noise
        out[name] = jnp.asarray(drawn.astype(out[name].dtype))
    for name, factor in factors.items():
        out[name] = (out[name] * factor).astype(out[name].dtype)
    return out
```

```python
from contextlib import ExitStack

import concourse.bass as bass
from concourse import mybir

ALU = mybir.AluOpType
ACT = mybir.ActivationFunctionType
AX = mybir.AxisListType
F32 = mybir.dt.float32
BF16 = mybir.dt.bfloat16
I32 = mybir.dt.int32

P = 128
EPS = 1e-5
NEG = -10000.0
K, V, Q = 0, 1, 2


def block_kernel(nc, x, ctx_in, mask, w_x, diag, w_in, b_in, w_out, b_out, g1, be1, g2, be2,
                 wg, w1, b1, w2, b2, out, xdisp, ydisp):
    L, N, D = x.shape
    S2 = ctx_in.shape[1]
    E, _, FF = w1.shape
    NJ = N // P
    T = L * NJ
    DC = D // P
    FT = FF // P
    H = 4
    HD = D // H
    CAP = L * N // E
    PW = L * D
    assert L == 2 and NJ == E and DC == 2 and FT == 8 and NJ % 2 == 0 and CAP == 2 * P

    with ExitStack() as ctx:
        def sb(name, shape, dt=F32):
            return ctx.enter_context(nc.sbuf_tensor(name, shape, dt))

        def sem(name):
            return ctx.enter_context(nc.semaphore(name))

        def bank(name):
            return ctx.enter_context(nc.psum_tensor(name, [P, 512], F32))

        x_sb = sb("x_sb", [P, NJ * PW])
        xb_sb = sb("xb_sb", [P, NJ * PW])
        y1_sb = x_sb
        yg_sb = sb("yg_sb", [P, NJ * PW])
        xn = sb("xn", [P, PW])
        xnT = sb("xnT", [P, DC, L * P])
        x1T = sb("x1T", [P, DC, L * P])
        shifted = sb("shifted", [P, L, S2])
        probs = sb("probs", [P, L, S2])
        probsT = sb("probsT", [S2, L * P])
        xres = sb("xres", [P, PW])
        h_sb = sb("h_sb", [P, 2, PW])
        hb = sb("hb", [P, 2, PW])
        hT = sb("hT", [P, DC, L * P])
        hdT = sb("hdT", [P, DC, P])
        kvd = sb("kvd", [P, 2 * D])
        qb = sb("qb", [P, PW])
        v1b = sb("v1b", [P, D])
        prod = sb("prod", [P, PW])
        o_sb = sb("o_sb", [P, PW])
        oT = sb("oT", [P, DC, L * P])
        r_sb = sb("r_sb", [P, PW])
        rg = sb("rg", [P, PW])
        y1 = sb("y1", [P, 2, PW])
        y1T = sb("y1T", [P, DC, L * P])
        st = {n: sb(f"stats_{n}", [P, L, 6]) for n in "xhyz"}
        mv = {n: sb(f"mv_{n}", [P, L, 2]) for n in "xhyz"}
        ve = {n: sb(f"vareps_{n}", [P, L]) for n in "xhyz"}
        rs = {n: sb(f"rstd_{n}", [P, L]) for n in "xhyz"}
        counts = sb("counts", [P, L])
        nmax = sb("nmax", [P, L])
        esum = sb("esum", [P, L])
        rsum = sb("rsum", [P, L])
        dsc = sb("dsc", [P, L * H])
        dm = sb("dm", [P, 2, L * H])
        pe2 = sb("pe2", [P, 2, L * H])
        psum2 = sb("psum2", [P, L * H])
        prec = sb("prec", [P, L * H])
        pr = sb("pr", [P, L * H])
        logits = sb("logits", [P, L, NJ, E])
        gmax = sb("gmax", [P, T])
        gsh = sb("gsh", [P, T, E])
        gex = sb("gex", [P, T, E])
        gsum = sb("gsum", [P, T])
        gate = sb("gate", [P, T])
        ismax = sb("ismax", [P, T, E])
        rank = sb("rank", [P, T, E])
        first = sb("first", [P, T])
        hot = sb("hot", [P, T, E], BF16)
        posh = sb("posh", [P, T, E])
        loc = sb("loc", [P, T])
        over = sb("over", [P, T])
        slotf = sb("slotf", [P, T])
        slot = sb("slot", [P, T], I32)
        raw = sb("raw", [P, 5 * DC, D])
        w_raw, win_raw, wo_raw = raw[:, 0:DC, :], raw[:, DC:4 * DC, :], raw[:, 4 * DC:5 * DC, :]
        wT = sb("wT", [P, DC, D])
        winT = sb("winT", [P, DC, 3 * D])
        woT = sb("woT", [P, DC, D])
        ctx_sb = sb("ctx_sb", [S2, L, D])
        ctxT = sb("ctxT", [P, DC, L * S2])
        x2n = sb("x2n", [P, DC, L * S2])
        mask_i = sb("mask_i", [P, L * S2], I32)
        nmask = sb("nmask", [P, L, S2])
        diag_sb = sb("diag_sb", [DC, P])
        ndcol = sb("ndcol", [P, DC])
        wg_sb = sb("wg_sb", [P, DC, E])
        b1_sb = sb("b1_sb", [E, FF])
        b1T = sb("b1T", [P, FT, E])
        w1_sb = sb("w1_sb", [P, 2, DC, FF])
        w2_sb = sb("w2_sb", [P, 2, FT, D])
        w1T = sb("w1T", [P, FT, D])
        w12 = sb("w12", [P, E * DC * D])
        b12t = sb("b12t", [P, D])
        b12p = sb("b12p", [P, E * D])
        b12 = raw[:, 0:E, :].rearrange("p e d -> p (e d)")
        rows = {n: sb(f"row_{n}", [P, D]) for n in ("bq", "bv", "bo", "g1", "be1", "g2", "be2")}
        b2row = sb("b2row", [P, E * D])
        ident = sb("ident", [P, P])
        ones = sb("ones", [P, P])
        onesb = sb("onesb", [P, P], BF16)
        before = sb("before", [P, P], BF16)
        rev = sb("rev", [P, E])
        epst = sb("epst", [P, L])
        mhalf = sb("mhalf", [P, L])
        zero = yg_sb[:, 0:2048]
        xe = w1_sb[:, :, :, :].rearrange("p a c f -> p (a c f)")
        xeT = w1T[:, 0:4, :].rearrange("p (b c) n -> p b c n", b=2)
        ye = w2_sb[:, :, :, :].rearrange("p a t d -> p (a t d)")
        zt, zg = h_sb, hb
        zo = x_sb

        TA, TB, WA, WB, AC, BQ, BV, BK = [bank(n) for n in
                                          ("tpA", "tpB", "w1tA", "w1tB", "w12acc", "psQ", "psVQ", "psKV")]

        s_xl0, s_xl1, s_xlr = sem("x0_loaded"), sem("x1_loaded"), sem("xrest_loaded")
        s_wx, s_ctx, s_win, s_wo = sem("wx_loaded"), sem("ctx_loaded"), sem("win_loaded"), sem("wo_loaded")
        s_small, s_rows, s_b2 = sem("small_loaded"), sem("rows_loaded"), sem("b2_loaded")
        s_w1 = [sem("w1_loaded0"), sem("w1_loaded1")]
        s_w2 = [sem("w2_loaded0"), sem("w2_loaded1")]
        s_const, s_ident0, s_tri, s_zero = sem("const_ready"), sem("ident_zeroed"), sem("tri_ready"), sem("zero_ready")
        s_wxT, s_woT, s_winT, s_ctxT, s_b1T = [sem(n) for n in ("wxT_psum", "woT_psum", "winT_psum", "ctxT_psum", "b1T_psum")]
        s_setT = sem("setup_transposes_copied")
        s_x2, s_x2n, s_dn, s_nm = sem("x2rep_psum"), sem("x2n_ready"), sem("ndcol_ready"), sem("nmask_step")
        s_xn, s_xnTp, s_xnT = sem("xn_ready"), sem("xnT_psum"), sem("xnT_copied")
        s_x1p, s_x1 = sem("x1rep_psum"), sem("x1rep_ready")
        s_scp, s_shift, s_probs = sem("scores_psum"), sem("shifted_ready"), sem("probs_ready")
        s_prTp, s_prT, s_attp, s_xres = sem("probsT_psum"), sem("probsT_copied"), sem("attended_psum"), sem("xres_ready")
        s_h, s_hTp, s_hT, s_hd = sem("h_ready"), sem("hT_psum"), sem("hT_copied"), sem("hdiffT_ready")
        s_qp, s_kp, s_kvd, s_qv = sem("q_v_psum"), sem("k_v_diff_psum"), sem("k_v_diff_copied"), sem("q_v_biased")
        s_pd, s_pe2, s_o = sem("score_diff_ready"), sem("pair_exp_ready"), sem("o_ready")
        s_oTp, s_oT, s_prp = sem("oT_psum"), sem("oT_copied"), sem("projected_psum")
        s_r, s_y1 = sem("r_ready"), sem("y1_ready")
        s_y1Tp, s_y1T, s_lgp, s_lg = sem("y1T_psum"), sem("y1T_copied"), sem("logits_psum"), sem("logits_copied")
        s_wTp, s_wT = sem("w1T_psum"), sem("w1T_copied")
        s_w12p, s_w12, s_bp, s_b12 = sem("w12_psum"), sem("w12_copied"), sem("b12_step"), sem("b12_accumulated")
        s_hb, s_xb, s_y1c = sem("hb_ready"), sem("xb_ready"), sem("y1_kept")
        s_ln = {n: sem(f"ln_{n}_step") for n in "xhyz"}
        s_var = {n: sem(f"var_{n}_ready") for n in "xhyz"}
        s_ve = {n: sem(f"vareps_{n}_ready") for n in "xhyz"}
        s_rs = {n: sem(f"rstd_{n}_ready") for n in "xhyz"}
        s_att = sem("attention_step")
        s_g, s_gsh, s_gex, s_hot, s_pos = sem("router_step"), sem("gate_shifted"), sem("gate_exp"), sem("onehot_ready"), sem("positions_psum")
        s_slot, s_gate = sem("slots_ready"), sem("gates_ready")
        s_b12s, s_b12p = sem("b12_parts_summed"), sem("b12_psum")
        s_b12r = sem("b12_ready")
        s_zd, s_scat, s_xe = sem("dispatch_zeroed"), sem("scattered"), [sem(f"xe_loaded{e}") for e in range(E)]
        s_xeTp, s_xeT, s_yep, s_ye = sem("xeT_psum"), sem("xeT_copied"), sem("ye_psum"), sem("ye_ready")
        s_yst = sem("ye_stored")
        s_yg = [sem(f"yg_gathered{j}") for j in range(NJ)]
        s_z, s_zo, s_out = sem("z_step"), sem("out_rows_ready"), sem("out_stored")

        x_t = x.rearrange("l (j p) d -> p l j d", p=P)
        x_v = x_sb[:, :].rearrange("p (j l d) -> p l j d", l=L, d=D)
        xe_rows = xdisp.rearrange("(e s p) d -> p e s d", s=2, p=P)
        ye_rows = ydisp.rearrange("(e s p) d -> p e s d", s=2, p=P)

        block = ctx.enter_context(nc.Block())

        def pair(t, j):
            return t[:, bass.ds(j * PW, PW)].rearrange("p (l d) -> p l d", l=L)

        def both(t):
            return t.rearrange("p (l d) -> p l d", l=L)

        @block.sync
        def _(sp):
            for l in range(L):
                sp.dma_start(x_v[:, l, 0:1, :], x_t[:, l, 0:1, :]).then_inc(s_xl0, 16)
            sp.dma_start(w_raw[:, :, :], w_x.rearrange("(c p) d -> p c d", p=P)).then_inc(s_wx, 16)
            sp.dma_start(ctx_sb[:, :, :], ctx_in.rearrange("l s d -> s l d")).then_inc(s_ctx, 16)
            sp.dma_start(w1_sb[:, 0, :, :], w1[0].rearrange("(c p) f -> p c f", p=P)).then_inc(s_w1[0], 16)
            sp.dma_start(w2_sb[:, 0, :, :], w2[0].rearrange("(t p) d -> p t d", p=P)).then_inc(s_w2[0], 16)
            for l in range(L):
                sp.dma_start(x_v[:, l, 1:2, :], x_t[:, l, 1:2, :]).then_inc(s_xl1, 16)
            sp.dma_start(win_raw[:, :, :], w_in.rearrange("(c p) d -> p c d", p=P)).then_inc(s_win, 16)
            sp.dma_start(wo_raw[:, :, :], w_out.rearrange("(c p) d -> p c d", p=P)).then_inc(s_wo, 16)
            sp.dma_start(w1_sb[:, 1, :, :], w1[1].rearrange("(c p) f -> p c f", p=P)).then_inc(s_w1[1], 16)
            sp.dma_start(w2_sb[:, 1, :, :], w2[1].rearrange("(t p) d -> p t d", p=P)).then_inc(s_w2[1], 16)
            for l in range(L):
                sp.dma_start(x_v[:, l, 2:NJ, :], x_t[:, l, 2:NJ, :]).then_inc(s_xlr, 16)
            with sp.Fori(1, NJ // 2) as i:
                for par in range(2):
                    e = i * 2 + par
                    sp.wait_ge(s_w12p, e - 1)
                    sp.dma_start(w1_sb[:, par, :, :], w1[bass.ds(e, 1)].rearrange("e (c p) f -> p (e c) f", p=P)).then_inc(s_w1[par], 16)
                    sp.wait_ge(s_b12, e - 1)
                    sp.dma_start(w2_sb[:, par, :, :], w2[bass.ds(e, 1)].rearrange("e (t p) d -> p (e t) d", p=P)).then_inc(s_w2[par], 16)
            sp.wait_ge(s_scat, 16 * T)
            for e in range(E):
                sp.dma_start(xe[:, e * 2 * D:(e + 1) * 2 * D].rearrange("p (s d) -> p s d", s=2), xe_rows[:, e]).then_inc(s_xe[e], 16)
            for e in range(E):
                sp.wait_ge(s_ye, e + 1)
                sp.dma_start(ye_rows[:, e], ye[:, e * 2 * D:(e + 1) * 2 * D].rearrange("p (s d) -> p s d", s=2)).then_inc(s_yst, 16)
            for j in range(NJ):
                sp.wait_ge(s_zo, j + 1)
                sp.dma_start(out.rearrange("l (j p) d -> p l j d", p=P)[:, :, j], both(zo[:, j * PW:(j + 1) * PW])).then_inc(s_out, 16)
            sp.wait_ge(s_out, 16 * NJ)

        @block.gpsimd
        def _(pool):
            pool.memset(ident[:, :], 0.0).then_inc(s_ident0, 1)
            pool.wait_ge(s_ident0, 1)
            pool.affine_select(out=ident[:, :], in_=ident[:, :], compare_op=ALU.not_equal, fill=1.0, base=0,
                               pattern=[[-1, P]], channel_multiplier=1).then_inc(s_const, 1)
            pool.memset(epst[:, :], EPS).then_inc(s_const, 1)
            pool.memset(mhalf[:, :], -0.5).then_inc(s_const, 1)
            pool.memset(zero[:, :], 0.0).then_inc(s_zero, 1)
            pool.memset(ones[:, :], 1.0).then_inc(s_const, 1)
            pool.memset(onesb[:, :], 1.0).then_inc(s_const, 1)
            pool.memset(before[:, :], 1.0).then_inc(s_tri, 1)
            pool.wait_ge(s_tri, 1)
            pool.affine_select(out=before[:, :], in_=before[:, :], compare_op=ALU.is_gt, fill=0.0, base=0,
                               pattern=[[1, P]], channel_multiplier=-1).then_inc(s_const, 1)
            for e in range(E):
                pool.memset(rev[:, e:e + 1], float(E - e)).then_inc(s_const, 1)
            pool.wait_ge(s_const, 6 + E)

            def rstd(n, j):
                pool.wait_ge(s_var[n], j + 1)
                pool.tensor_tensor(ve[n][:, :], mv[n][:, :, 1], epst[:, :], ALU.add).then_inc(s_ve[n], 1)
                pool.wait_ge(s_ve[n], j + 1)
                pool.tensor_tensor(rs[n][:, :], ve[n][:, :], mhalf[:, :], ALU.pow).then_inc(s_rs[n], 1)

            def step(j, par, cross, proj, ahead):
                if ahead:
                    rstd("x", j + 1)
                if proj:
                    rstd("y", j - 2)
                if cross:
                    rstd("h", j)
                    pool.wait_ge(s_xres, j * L + L)
                    pool.tensor_tensor(pair(xb_sb, j), both(xres[:, :]), rows["be2"][:, :].unsqueeze(1).broadcast_to([P, L, D]), ALU.add).then_inc(s_xb, 1)
                    pool.wait_ge(s_h, j + 1)
                    pool.tensor_tensor(both(hb[:, par, :]), both(h_sb[:, par % 2, :]), rows["bo"][:, :].unsqueeze(1).broadcast_to([P, L, D]), ALU.add).then_inc(s_hb, 1)

            rstd("x", 0)
            pool.wait_ge(s_rows, 16 * 7)
            step(0, 0, True, False, True)
            pool.memset(yg_sb[:, 2048:], 0.0).then_inc(s_zero, 1)
            step(1, 1, True, False, True)
            with pool.Fori(1, NJ // 2 - 1) as i:
                for par in range(2):
                    step(i * 2 + par, par, True, True, True)
            step(NJ - 2, 0, True, True, True)
            step(NJ - 1, 1, True, True, False)
            step(NJ, 0, False, True, False)
            step(NJ + 1, 1, False, True, False)
            pool.wait_ge(s_zd, 32)
            pool.wait_ge(s_y1c, NJ)
            pool.wait_ge(s_slot, 1)
            for t in range(T):
                l, j = divmod(t, NJ)
                pool.indirect_dma_start(out=xdisp, out_offset=bass.IndirectOffsetOnAxis(ap=slot[:, t:t + 1], axis=0),
                                        in_=y1_sb[:, j * PW + l * D:j * PW + (l + 1) * D], in_offset=None,
                                        bounds_check=E * CAP - 1, oob_is_err=False).then_inc(s_scat, 16)
            pool.wait_ge(s_zero, 2)
            pool.wait_ge(s_yst, 16 * E)

            def gather(j):
                for l in range(L):
                    t = l * NJ + j
                    pool.indirect_dma_start(out=yg_sb[:, j * PW + l * D:j * PW + (l + 1) * D], out_offset=None,
                                            in_=ydisp, in_offset=bass.IndirectOffsetOnAxis(ap=slot[:, t:t + 1], axis=0),
                                            bounds_check=E * CAP - 1, oob_is_err=False).then_inc(s_yg[j], 16)

            gather(0)
            gather(1)
            for j in range(NJ):
                if j + 2 < NJ:
                    gather(j + 2)
                rstd("z", j)

        @block.scalar
        def _(act):
            act.dma_start(mask_i[:, :], mask.rearrange("l s -> (l s)").partition_broadcast(P)).then_inc(s_small, 16)
            act.dma_start(diag_sb[:, :], diag.rearrange("(c p) -> c p", p=P)).then_inc(s_small, 16)
            act.dma_start(wg_sb[:, :, :], wg.rearrange("(c p) e -> p c e", p=P)).then_inc(s_small, 16)
            act.dma_start(b1_sb[:, :], b1).then_inc(s_small, 16)
            for n, v in (("bq", b_in[0:D]), ("bv", b_in[2 * D:3 * D]), ("bo", b_out), ("g1", g1), ("be1", be1), ("g2", g2), ("be2", be2)):
                act.dma_start(rows[n][:, :], v.partition_broadcast(P)).then_inc(s_rows, 16)
            act.dma_start(b2row[:, :], b2.rearrange("e d -> (e d)").partition_broadcast(P)).then_inc(s_b2, 16)
            act.wait_ge(s_zero, 1)
            for half in range(2):
                act.dma_start(xdisp[half * 1024:(half + 1) * 1024].rearrange("(p r) d -> p (r d)", p=P), zero[:, :]).then_inc(s_zd, 16)

            def copy(dst, src, done):
                act.activation(dst, src, ACT.Copy).then_inc(done, 1)

            act.wait_ge(s_wxT, 1)
            copy(wT[:, :, :].rearrange("p c h -> p (c h)"), TB[:, :], s_setT)
            act.wait_ge(s_ctxT, 1)
            copy(ctxT[:, :, :].rearrange("p c s -> p (c s)"), WA[:, 0:DC * L * S2], s_setT)
            act.wait_ge(s_b1T, 1)
            copy(b1T[:, :, :].rearrange("p t e -> p (t e)"), AC[:, 0:FT * E], s_setT)
            act.activation(ndcol[:, :], AC[:, FT * E:FT * E + DC], ACT.Copy, scale=-1.0).then_inc(s_dn, 1)
            act.wait_ge(s_winT, 3)
            for n, b in enumerate((BQ, BV, BK)):
                copy(winT[:, :, n * D:(n + 1) * D], b[:, :].rearrange("p (c o) -> p c o", c=DC), s_lg if b is BK else s_setT)
            act.wait_ge(s_woT, 1)
            copy(woT[:, :, :].rearrange("p c o -> p (c o)"), TA[:, :], s_y1T)

            def w1T_copy(j, k):
                act.wait_ge(s_wTp, j * 4 + (k + 1))
                b = (WA, WB)[k % 2]
                copy(w1T[:, 2 * k:2 * k + 2, :].rearrange("p t d -> p (t d)"), b[:, :], s_wT)

            def step(j, par, cross, attn, proj):
                if cross:
                    w1T_copy(j, 0)
                    w1T_copy(j, 1)
                if attn:
                    act.wait_ge(s_hTp, j)
                    copy(hT[:, :, :].rearrange("p c n -> p (c n)"), TA[:, :], s_hT)
                if cross:
                    act.wait_ge(s_xnTp, j + 1)
                    copy(xnT[:, :, :].rearrange("p c n -> p (c n)"), TB[:, :], s_xnT)
                if proj:
                    act.wait_ge(s_oTp, j - 1)
                    copy(oT[:, :, :].rearrange("p c n -> p (c n)"), TA[:, :], s_oT)
                if cross:
                    act.wait_ge(s_x1p, j + 1)
                    act.activation(x1T[:, :, :].rearrange("p c n -> p (c n)"), TB[:, :], ACT.Relu).then_inc(s_x1, 1)
                if attn:
                    act.wait_ge(s_kp, j)
                    copy(kvd[:, :], BK[:, :], s_kvd)
                if cross:
                    w1T_copy(j, 2)
                    w1T_copy(j, 3)
                    act.wait_ge(s_shift, j + 1)
                    for l in range(L):
                        last = act.activation(probs[:, l, :], shifted[:, l, :], ACT.Exp, scale=-1.0,
                                              bias=nmax[:, l:l + 1], accum_out=esum[:, l:l + 1])
                    last.then_inc(s_probs, 1)
                    act.wait_ge(s_prTp, j + 1)
                    copy(probsT[:, :], TB[0:S2, 256:512], s_prT)
                if attn:
                    act.wait_ge(s_pd, j)
                    act.activation(pe2[:, :, :], dm[:, :, :], ACT.Exp, scale=HD ** -0.5).then_inc(s_pe2, 1)
                if proj:
                    act.wait_ge(s_y1Tp, j - 1)
                    copy(y1T[:, :, :].rearrange("p c n -> p (c n)"), TA[:, :], s_y1T)
                    copy(y1_sb[:, bass.ds((j - 2) * PW, PW)], y1[:, par, :], s_y1c)
                if cross:
                    act.wait_ge(s_w12p, j + 1)
                    copy(w12[:, bass.ds(j * (DC * D), DC * D)], AC[:, :], s_w12)

            step(0, 0, True, False, False)
            step(1, 1, True, True, False)
            with act.Fori(1, NJ // 2) as i:
                for par in range(2):
                    step(i * 2 + par, par, True, True, True)
            step(NJ, 0, False, True, True)
            step(NJ + 1, 1, False, False, True)
            act.wait_ge(s_gsh, 1)
            act.activation(gex[:, :, :], gsh[:, :, :], ACT.Exp).then_inc(s_gex, 1)
            for e in range(E):
                act.wait_ge(s_xeTp, e + 1)
                copy(xeT[:, e % 2, :, :].rearrange("p c n -> p (c n)"), (TA, TB)[e % 2][:, :], s_xeT)

        @block.vector
        def _(dve):
            def norm_stats(n, src, j, steps, at):
                for l in range(L):
                    dve.bn_stats(st[n][:, l, :], src[:, l, :]).then_inc(s_ln[n], 1)
                dve.wait_ge(s_ln[n], j * steps + (at + L))
                dve.tensor_copy(counts[:, :], st[n][:, :, 0])
                for l in range(L):
                    last = dve.bn_aggr(mv[n][:, l, :], st[n][:, l, :])
                last.then_inc(s_var[n], 1)
                dve.wait_ge(s_rs[n], j + 1)

            def normed(n, dst, src, l):
                return dve.tensor_scalar(dst, src, mv[n][:, l, 0:1], rs[n][:, l:l + 1], ALU.subtract, ALU.mult)

            dve.wait_ge(s_small, 64)
            dve.tensor_scalar(nmask[:, :, :].rearrange("p l s -> p (l s)"), mask_i[:, :], 1.0, NEG, ALU.subtract, ALU.mult).then_inc(s_nm, 1)
            dve.wait_ge(s_dn, 1)
            dve.wait_ge(s_nm, 1)

            def cross_in(j):
                norm_stats("x", pair(x_sb, j), j, 2, 0)
                for l in range(L):
                    last = normed("x", xn[:, l * D:(l + 1) * D], x_sb[:, bass.ds(j * PW + l * D, D)], l)
                last.then_inc(s_xn, 1)

            def scores_shift(j):
                dve.wait_ge(s_nm, 1)
                dve.wait_ge(s_scp, j + 1)
                for l in range(L):
                    last = dve.tensor_tensor_reduce(out=shifted[:, l, :], in0=TB[:, l * S2:(l + 1) * S2], in1=nmask[:, l, :],
                                                    scale=1.0, scalar=3.0e38, op0=ALU.add, op1=ALU.min, accum_out=nmax[:, l:l + 1])
                last.then_inc(s_shift, 1)

            def cross_out(j, par):
                dve.wait_ge(s_probs, j + 1)
                dve.reciprocal(rsum[:, :], esum[:, :]).then_inc(s_ln["h"], 1)
                dve.wait_ge(s_attp, j + 1)
                if not isinstance(j, int) or j > 0:
                    dve.wait_ge(s_xb, j)
                dve.wait_ge(s_ln["h"], j * 3 + 1)
                for l in range(L):
                    dve.scalar_tensor_tensor(xres[:, l * D:(l + 1) * D], TB[:, l * D:(l + 1) * D], rsum[:, l:l + 1],
                                             x_sb[:, bass.ds(j * PW + l * D, D)], ALU.mult, ALU.add).then_inc(s_xres, 1)
                dve.wait_ge(s_xres, j * L + L)
                norm_stats("h", both(xres[:, :]), j, 3, 1)
                if not isinstance(j, int) or j > 1:
                    dve.wait_ge(s_hb, j - 1)
                for l in range(L):
                    last = normed("h", h_sb[:, par, l * D:(l + 1) * D], xres[:, l * D:(l + 1) * D], l)
                last.then_inc(s_h, 1)

            def diff(j):
                dve.wait_ge(s_hT, j)
                dve.tensor_tensor(hdT[:, :, :], hT[:, :, 0:P], hT[:, :, P:2 * P], ALU.subtract).then_inc(s_hd, 1)

            NATT = 10

            def attention_a(j):
                base = (j - 1) * NATT
                dve.wait_ge(s_qp, j)
                dve.tensor_tensor(qb[:, 0:D], BQ[:, 0:D], rows["bq"][:, :], ALU.add).then_inc(s_att, 1)
                dve.tensor_tensor(qb[:, D:2 * D], BV[:, D:2 * D], rows["bq"][:, :], ALU.add).then_inc(s_att, 1)
                dve.tensor_tensor(v1b[:, :], BV[:, 0:D], rows["bv"][:, :], ALU.add).then_inc(s_qv, 1)
                dve.wait_ge(s_kvd, j)
                dve.wait_ge(s_att, base + 2)
                dve.tensor_tensor(both(prod[:, :]), both(qb[:, :]), kvd[:, 0:D].unsqueeze(1).broadcast_to([P, L, D]), ALU.mult).then_inc(s_att, 1)
                dve.wait_ge(s_att, base + 3)
                dve.tensor_reduce(dsc[:, :], prod[:, :].rearrange("p (g d) -> p g d", d=HD), AX.X, ALU.add).then_inc(s_att, 1)
                dve.wait_ge(s_att, base + 4)
                dve.tensor_scalar(dm[:, 0, :], dsc[:, :], 0.0, None, ALU.min).then_inc(s_att, 1)
                dve.tensor_scalar(dm[:, 1, :], dsc[:, :], -1.0, 0.0, ALU.mult, ALU.min).then_inc(s_pd, 1)

            def attention_b(j):
                base = (j - 1) * NATT
                dve.wait_ge(s_pe2, j)
                dve.tensor_tensor(psum2[:, :], pe2[:, 0, :], pe2[:, 1, :], ALU.add).then_inc(s_att, 1)
                dve.wait_ge(s_att, base + 6)
                dve.reciprocal(prec[:, :], psum2[:, :]).then_inc(s_att, 1)
                dve.wait_ge(s_att, base + 7)
                dve.tensor_tensor(pr[:, :], pe2[:, 0, :], prec[:, :], ALU.mult).then_inc(s_att, 1)
                dve.wait_ge(s_att, base + 8)
                for l in range(L):
                    dve.tensor_tensor(prod[:, l * D:(l + 1) * D].rearrange("p (h d) -> p h d", d=HD),
                                             kvd[:, D:2 * D].rearrange("p (h d) -> p h d", d=HD),
                                             pr[:, l * H:(l + 1) * H].unsqueeze(2).broadcast_to([P, H, HD]), ALU.mult).then_inc(s_att, 1)
                dve.wait_ge(s_att, base + 10)
                if not isinstance(j, int) or j > 1:
                    dve.wait_ge(s_oTp, j - 1)
                for l in range(L):
                    dve.tensor_tensor(o_sb[:, l * D:(l + 1) * D], prod[:, l * D:(l + 1) * D], v1b[:, :], ALU.add).then_inc(s_o, 1)

            def project(j, par):
                dve.wait_ge(s_prp, j - 1)
                dve.wait_ge(s_hb, j - 1)
                dve.tensor_tensor(r_sb[:, :], TA[:, :], hb[:, par, :], ALU.add).then_inc(s_r, 1)
                dve.wait_ge(s_r, j - 1)
                norm_stats("y", both(r_sb[:, :]), j - 2, 4, 0)
                for l in range(L):
                    dve.scalar_tensor_tensor(rg[:, l * D:(l + 1) * D], r_sb[:, l * D:(l + 1) * D], mv["y"][:, l, 0:1],
                                             rows["g1"][:, :], ALU.subtract, ALU.mult).then_inc(s_ln["y"], 1)
                dve.wait_ge(s_ln["y"], (j - 2) * 4 + 4)
                for l in range(L):
                    last = dve.scalar_tensor_tensor(y1[:, par, l * D:(l + 1) * D], rg[:, l * D:(l + 1) * D], rs["y"][:, l:l + 1],
                                                    rows["be1"][:, :], ALU.mult, ALU.add)
                last.then_inc(s_y1, 1)

            def logits_copy(j):
                dve.wait_ge(s_lgp, j - 1)
                dve.tensor_copy(logits[:, :, bass.ds(j - 2, 1), :].rearrange("p l j e -> p (l j) e"),
                                BK[:, 0:L * E].rearrange("p (l e) -> p l e", l=L)).then_inc(s_lg, 1)

            def bias_sum(e, half, par):
                dve.wait_ge(s_w2[par], half * 16 + 16)
                odd = b12p[:, bass.ds(e * D, D)]
                for k in range(FT):
                    acc = (b12t[:, :], odd)[k % 2]
                    if k < 2:
                        ins = dve.tensor_scalar(acc, w2_sb[:, par, k, :], b1T[:, k, bass.ds(e, 1)], None, ALU.mult)
                    else:
                        dve.wait_ge(s_bp, e * FT + (k - 1))
                        ins = dve.scalar_tensor_tensor(acc, w2_sb[:, par, k, :], b1T[:, k, bass.ds(e, 1)], acc, ALU.mult, ALU.add)
                    ins.then_inc(s_bp, 1)
                dve.wait_ge(s_bp, e * FT + FT)
                dve.tensor_tensor(odd, odd, b12t[:, :], ALU.add).then_inc(s_b12, 1)

            def step(j, half, par, cross, attn, proj, ahead):
                if attn:
                    diff(j)
                if ahead:
                    dve.wait_ge(s_xnTp, j + 1)
                    cross_in(j + 1)
                if cross:
                    bias_sum(j, half, par)
                if proj:
                    project(j, par)
                if cross:
                    scores_shift(j)
                if attn:
                    attention_a(j)
                if cross:
                    cross_out(j, par)
                if attn:
                    attention_b(j)
                if proj:
                    logits_copy(j)

            dve.wait_ge(s_xl0, 16 * L)
            cross_in(0)
            dve.wait_ge(s_x2, 1)
            for c in range(DC):
                last = dve.tensor_scalar(x2n[:, c, :], WB[:, c * L * S2:(c + 1) * L * S2], 0.0, ndcol[:, c:c + 1], ALU.max, ALU.mult)
            last.then_inc(s_x2n, 1)
            dve.wait_ge(s_xl1, 16 * L)
            dve.wait_ge(s_setT, 3)
            step(0, 0, 0, True, False, False, True)
            dve.wait_ge(s_rows, 16 * 7)
            dve.wait_ge(s_xlr, 16 * L)
            step(1, 0, 1, True, True, False, True)
            with dve.Fori(1, NJ // 2 - 1) as i:
                for par in range(2):
                    step(i * 2 + par, i, par, True, True, True, True)
            step(NJ - 2, NJ // 2 - 1, 0, True, True, True, True)
            step(NJ - 1, NJ // 2 - 1, 1, True, True, True, False)
            step(NJ, 0, 0, False, True, True, False)
            step(NJ + 1, 0, 1, False, False, True, False)

            n = [0]

            def then(ins):
                n[0] += 1
                ins.then_inc(s_g, 1)
                dve.wait_ge(s_g, n[0])

            lg = logits[:, :, :, :].rearrange("p l j e -> p (l j) e")
            wide = lambda t: t.unsqueeze(2).broadcast_to([P, T, E])
            revb = rev[:, :].unsqueeze(1).broadcast_to([P, T, E])
            dve.wait_ge(s_lg, NJ + 1)
            then(dve.tensor_reduce(gmax[:, :], lg, AX.X, ALU.max))
            then(dve.tensor_tensor(ismax[:, :, :], lg, wide(gmax[:, :]), ALU.is_ge))
            then(dve.tensor_tensor(rank[:, :, :], ismax[:, :, :], revb, ALU.mult))
            then(dve.tensor_reduce(first[:, :], rank[:, :, :], AX.X, ALU.max))
            dve.tensor_tensor(hot[:, :, :], revb, wide(first[:, :]), ALU.is_equal).then_inc(s_hot, 1)
            dve.tensor_tensor(gsh[:, :, :], lg, wide(gmax[:, :]), ALU.subtract).then_inc(s_gsh, 1)
            dve.wait_ge(s_hot, 1)
            dve.wait_ge(s_pos, 1)
            then(dve.tensor_tensor(posh[:, :, :], AC[:, 0:T * E].rearrange("p (t e) -> p t e", e=E), hot[:, :, :], ALU.mult))
            then(dve.tensor_reduce(loc[:, :], posh[:, :, :], AX.X, ALU.add))
            dve.tensor_scalar(over[:, :], loc[:, :], float(CAP), float(2 * E * CAP), ALU.is_ge, ALU.mult).then_inc(s_g, 1)
            n[0] += 1
            then(dve.scalar_tensor_tensor(slotf[:, :], first[:, :], -float(CAP), loc[:, :], ALU.mult, ALU.add))
            dve.scalar_tensor_tensor(slot[:, :], slotf[:, :], float(E * CAP), over[:, :], ALU.add, ALU.add).then_inc(s_slot, 1)
            dve.wait_ge(s_gex, 1)
            then(dve.tensor_reduce(gsum[:, :], gex[:, :, :], AX.X, ALU.add))
            dve.reciprocal(gate[:, :], gsum[:, :]).then_inc(s_gate, 1)
            dve.wait_ge(s_b2, 16)
            for k, b in enumerate((WA, WB, BV, BK)):
                dve.wait_ge(s_b12p, k + 1)
                dve.tensor_tensor(b12[:, k * 512:(k + 1) * 512], b[:, :], b2row[:, k * 512:(k + 1) * 512], ALU.add).then_inc(s_b12r, 1)
            dve.wait_ge(s_b12r, 4)
            for e in range(E):
                dve.wait_ge(s_yep, e + 1)
                dve.tensor_tensor(ye[:, e * 2 * D:(e + 1) * 2 * D].rearrange("p (s d) -> p s d", s=2),
                                  (BV, BK)[e % 2][:, :].rearrange("p (s d) -> p s d", s=2),
                                  b12[:, e * D:(e + 1) * D].unsqueeze(1).broadcast_to([P, 2, D]), ALU.add).then_inc(s_ye, 1)
            dve.wait_ge(s_gate, 1)
            dve.wait_ge(s_xb, NJ)
            for j in range(NJ):
                b = j % 2
                dve.wait_ge(s_yg[j], 16 * L)
                for l in range(L):
                    t = l * NJ + j
                    c = j * PW + l * D
                    dve.scalar_tensor_tensor(zt[:, b, l * D:(l + 1) * D], yg_sb[:, c:c + D], gate[:, t:t + 1], y1_sb[:, c:c + D], ALU.mult, ALU.add).then_inc(s_z, 1)
                dve.wait_ge(s_z, j * 4 + 2)
                norm_stats("z", both(zt[:, b, :]), j, 2, 0)
                for l in range(L):
                    dve.scalar_tensor_tensor(zg[:, b, l * D:(l + 1) * D], zt[:, b, l * D:(l + 1) * D], mv["z"][:, l, 0:1], rows["g2"][:, :], ALU.subtract, ALU.mult).then_inc(s_z, 1)
                dve.wait_ge(s_z, j * 4 + 4)
                for l in range(L):
                    c = j * PW + l * D
                    last = dve.scalar_tensor_tensor(zo[:, c:c + D], zg[:, b, l * D:(l + 1) * D], rs["z"][:, l:l + 1], xb_sb[:, c:c + D], ALU.mult, ALU.add)
                last.then_inc(s_zo, 1)

        @block.tensor
        def _(pe):
            pe.wait_ge(s_const, 6 + E)
            pe.wait_ge(s_wx, 16)
            for c in range(DC):
                for h in range(DC):
                    last = pe.transpose(TB[:, c * D + h * P:c * D + (h + 1) * P], w_raw[:, h, c * P:(c + 1) * P], ident[:, :])
            last.then_inc(s_wxT, 1)
            pe.wait_ge(s_ctx, 16)
            for c in range(DC):
                for l in range(L):
                    last = pe.transpose(WA[:, (c * L + l) * S2:(c * L + l + 1) * S2], ctx_sb[:, l, c * P:(c + 1) * P], ident[0:S2, 0:S2])
            last.then_inc(s_ctxT, 1)
            pe.wait_ge(s_small, 64)
            for t in range(FT):
                last = pe.transpose(AC[:, t * E:(t + 1) * E], b1_sb[:, t * P:(t + 1) * P], ident[0:E, 0:E])
            pe.transpose(AC[:, FT * E:FT * E + DC], diag_sb[:, :], ident[0:DC, 0:DC]).then_inc(s_b1T, 1)
            pe.wait_ge(s_setT, 2)
            for h in range(DC):
                for c in range(DC):
                    last = pe.matmul(WB[:, h * L * S2:(h + 1) * L * S2], wT[:, c, h * P:(h + 1) * P], ctxT[:, c, :], start=(c == 0), stop=(c == DC - 1))
            last.then_inc(s_x2, 1)
            pe.wait_ge(s_win, 16)
            for n, b in enumerate((BQ, BV, BK)):
                for c in range(DC):
                    for a in range(DC):
                        o = ((n + 1) % 3) * DC + a
                        last = pe.transpose(b[:, c * D + a * P:c * D + (a + 1) * P], win_raw[:, o, c * P:(c + 1) * P], ident[:, :])
                last.then_inc(s_winT, 1)
            pe.wait_ge(s_wo, 16)
            for c in range(DC):
                for a in range(DC):
                    last = pe.transpose(TA[:, c * D + a * P:c * D + (a + 1) * P], wo_raw[:, a, c * P:(c + 1) * P], ident[:, :])
            last.then_inc(s_woT, 1)
            pe.wait_ge(s_x2n, 1)
            pe.wait_ge(s_setT, 5)
            pe.wait_ge(s_y1T, 1)
            pe.wait_ge(s_lg, 1)
            pe.wait_ge(s_dn, 1)

            def w1_transpose(j, k, par):
                b = (WA, WB)[k % 2]
                if k >= 2:
                    pe.wait_ge(s_wT, j * 4 + (k - 1))
                for a in range(2):
                    for c in range(DC):
                        last = pe.transpose(b[:, a * D + c * P:a * D + (c + 1) * P], w1_sb[:, par, c, (2 * k + a) * P:(2 * k + a + 1) * P], ident[:, :])
                last.then_inc(s_wTp, 1)

            def w12_part(c, t0, t1, par):
                for t in range(t0, t1):
                    last = pe.matmul(AC[:, c * D:(c + 1) * D], w1T[:, t, c * P:(c + 1) * P], w2_sb[:, par, t, :], start=(t == 0), stop=(t == FT - 1))
                return last

            def transposes(b, src):
                for c in range(DC):
                    for l in range(L):
                        last = pe.transpose(b[:, (c * L + l) * P:(c * L + l + 1) * P], src[:, l * D + c * P:l * D + (c + 1) * P], ident[:, :])
                return last

            def step(j, half, par, cross, attn, proj, attn_has_before=True):
                if cross:
                    pe.wait_ge(s_w1[par], half * 16 + 16)
                    if isinstance(j, int) and j == 0:
                        pass
                    else:
                        pe.wait_ge(s_wT, j * 4)
                    w1_transpose(j, 0, par)
                    w1_transpose(j, 1, par)
                if attn:
                    pe.wait_ge(s_h, j)
                    if attn_has_before:
                        pe.wait_ge(s_y1T, j - 1)
                    transposes(TA, h_sb[:, (par + 1) % 2, :]).then_inc(s_hTp, 1)
                if cross:
                    pe.wait_ge(s_xn, j + 1)
                    if not isinstance(j, int) or j > 0:
                        pe.wait_ge(s_xres, j * L)
                    transposes(TB, xn[:, :]).then_inc(s_xnTp, 1)
                    pe.wait_ge(s_w2[par], half * 16 + 16)
                    if not isinstance(j, int) or j > 0:
                        pe.wait_ge(s_w12, j)
                    pe.wait_ge(s_wT, j * 4 + 1)
                    w12_part(0, 0, 2, par)
                if proj:
                    pe.wait_ge(s_o, j * L - L)
                    if attn:
                        pe.wait_ge(s_hT, j)
                    else:
                        pe.wait_ge(s_y1T, j - 1)
                    transposes(TA, o_sb[:, :]).then_inc(s_oTp, 1)
                if attn:
                    pe.wait_ge(s_hT, j)
                    if not isinstance(j, int) or j > 1:
                        pe.wait_ge(s_qv, j - 1)
                    for c in range(DC):
                        pe.matmul(BQ[:, 0:D], hT[:, c, 0:P], winT[:, c, Q * D:(Q + 1) * D], start=(c == 0), stop=(c == DC - 1))
                    for c in range(DC):
                        last = pe.matmul(BV[:, :], hT[:, c, P:2 * P], winT[:, c, V * D:(Q + 1) * D], start=(c == 0), stop=(c == DC - 1))
                    last.then_inc(s_qp, 1)
                if cross:
                    pe.wait_ge(s_xnT, j + 1)
                    for h in range(DC):
                        for c in range(DC):
                            last = pe.matmul(TB[:, h * L * P:(h + 1) * L * P], wT[:, c, h * P:(h + 1) * P], xnT[:, c, :], start=(c == 0), stop=(c == DC - 1))
                    last.then_inc(s_x1p, 1)
                if attn:
                    pe.wait_ge(s_hd, j)
                    if not isinstance(j, int) or j > 1:
                        pe.wait_ge(s_kvd, j - 1)
                    if attn_has_before:
                        pe.wait_ge(s_lg, j - 1)
                    for c in range(DC):
                        last = pe.matmul(BK[:, :], hdT[:, c, :], winT[:, c, K * D:(V + 1) * D], start=(c == 0), stop=(c == DC - 1))
                    last.then_inc(s_kp, 1)
                if proj:
                    pe.wait_ge(s_oT, j - 1)
                    for l in range(L):
                        for c in range(DC):
                            last = pe.matmul(TA[:, l * D:(l + 1) * D], oT[:, c, l * P:(l + 1) * P], woT[:, c, :], start=(c == 0), stop=(c == DC - 1))
                    last.then_inc(s_prp, 1)
                if cross:
                    w1_transpose(j, 2, par)
                    w1_transpose(j, 3, par)
                    w12_part(0, 2, 4, par)
                    pe.wait_ge(s_x1, j + 1)
                    for l in range(L):
                        for c in range(DC):
                            last = pe.matmul(TB[:, l * S2:(l + 1) * S2], x1T[:, c, l * P:(l + 1) * P], x2n[:, c, l * S2:(l + 1) * S2], start=(c == 0), stop=(c == DC - 1))
                    last.then_inc(s_scp, 1)
                    pe.wait_ge(s_wT, j * 4 + 4)
                    w12_part(0, 4, 8, par)
                    pe.wait_ge(s_probs, j + 1)
                    for l in range(L):
                        last = pe.transpose(TB[0:S2, 256 + l * P:256 + (l + 1) * P], probs[:, l, :], ident[:, :])
                    last.then_inc(s_prTp, 1)
                    w12_part(1, 0, 4, par)
                    pe.wait_ge(s_prT, j + 1)
                    for l in range(L):
                        last = pe.matmul(TB[:, l * D:(l + 1) * D], probsT[:, l * P:(l + 1) * P], ctx_sb[:, l, :], start=True, stop=True)
                    last.then_inc(s_attp, 1)
                if proj:
                    pe.wait_ge(s_y1, j - 1)
                    for c in range(DC):
                        for l in range(L):
                            last = pe.transpose(TA[:, (c * L + l) * P:(c * L + l + 1) * P], y1[:, par, l * D + c * P:l * D + (c + 1) * P], ident[:, :])
                    last.then_inc(s_y1Tp, 1)
                if cross:
                    w12_part(1, 4, 8, par).then_inc(s_w12p, 1)
                if proj:
                    pe.wait_ge(s_y1T, j)
                    if attn:
                        pe.wait_ge(s_kvd, j)
                    else:
                        pe.wait_ge(s_lg, j - 1)
                    for l in range(L):
                        for c in range(DC):
                            last = pe.matmul(BK[:, l * E:(l + 1) * E], y1T[:, c, l * P:(l + 1) * P], wg_sb[:, c, :], start=(c == 0), stop=(c == DC - 1))
                    last.then_inc(s_lgp, 1)

            step(0, 0, 0, True, False, False, False)
            step(1, 0, 1, True, True, False, False)
            with pe.Fori(1, NJ // 2) as i:
                for par in range(2):
                    step(i * 2 + par, i, par, True, True, True)
            step(NJ, 0, 0, False, True, True)
            step(NJ + 1, 0, 1, False, False, True)

            pe.wait_ge(s_hot, 1)
            pe.wait_ge(s_w12, NJ)
            pe.matmul(AC[:, 0:T * E], before[:, :], hot[:, :, :].rearrange("p t e -> p (t e)"), start=True, stop=False)
            for t in range(T - 1):
                last = pe.matmul(AC[:, (t + 1) * E:T * E].rearrange("p (t e) -> p t e", e=E), onesb[:, :],
                                 hot[:, t:t + 1, :].broadcast_to([P, T - 1 - t, E]), start=False, stop=(t == T - 2))
            last.then_inc(s_pos, 1)
            pe.wait_ge(s_b12, E)
            pe.wait_ge(s_wT, 4 * E)
            pe.wait_ge(s_qv, NJ)
            pe.wait_ge(s_kvd, NJ)
            for k, b in enumerate((WA, WB, BV, BK)):
                pe.matmul(b[:, :], ones[:, :], b12p[:, k * 512:(k + 1) * 512], start=True, stop=True).then_inc(s_b12p, 1)

            def slots_transposed(e):
                pe.wait_ge(s_xe[e], 16)
                for c in range(DC):
                    for s in range(2):
                        last = pe.transpose((TA, TB)[e % 2][:, (c * 2 + s) * P:(c * 2 + s + 1) * P],
                                            xe[:, (e * 2 + s) * D + c * P:(e * 2 + s) * D + (c + 1) * P], ident[:, :])
                last.then_inc(s_xeTp, 1)

            pe.wait_ge(s_b12r, 4)
            slots_transposed(0)
            for e in range(E):
                if e + 1 < E:
                    slots_transposed(e + 1)
                pe.wait_ge(s_xeT, e + 1)
                if e >= 2:
                    pe.wait_ge(s_ye, e - 1)
                for s in range(2):
                    for c in range(DC):
                        last = pe.matmul((BV, BK)[e % 2][:, s * D:(s + 1) * D], xeT[:, e % 2, c, s * P:(s + 1) * P],
                                         w12[:, (e * DC + c) * D:(e * DC + c + 1) * D], start=(c == 0), stop=(c == DC - 1))
                last.then_inc(s_yep, 1)


_INS = ["x", "ctx_1024", "mask_BxS2_if1", "L0_xattn_W", "L0_xattn_diagonal", "L0_ffn_in_proj_w", "L0_ffn_in_proj_b",
        "L0_ffn_out_proj_w", "L0_ffn_out_proj_b", "L0_ffn_ln1_g", "L0_ffn_ln1_b", "L0_ffn_ln2_g", "L0_ffn_ln2_b",
        "L0_ffn_wg", "L0_ffn_w1", "L0_ffn_b1", "L0_ffn_w2", "L0_ffn_b2"]


def kernel(**inputs):
    import numpy as np
    import concourse.bacc as bacc
    from concourse.bass_utils import run_bass_kernel_spmd as run

    nc = bacc.Bacc("TRN2", target_bir_lowering=False, num_devices=1)
    arrays, args = {}, []
    for name in _INS:
        a = np.ascontiguousarray(inputs[name])
        arrays["in_" + name] = a
        args.append(nc.dram_tensor("in_" + name, a.shape, mybir.dt.from_np(a.dtype), kind="ExternalInput").ap())
    shape = inputs["x"].shape
    args.append(nc.dram_tensor("out_x", shape, F32, kind="ExternalOutput").ap())
    rows = [shape[0] * shape[1], shape[2]]
    args.append(nc.dram_tensor("slots_in", rows, F32, kind="Internal").ap())
    args.append(nc.dram_tensor("slots_out", rows, F32, kind="Internal").ap())
    block_kernel(nc, *args)
    r = run(nc, [arrays], core_ids=[0])
    return r.results[0]["out_x"]
```

```python
from contextlib import ExitStack

import concourse.bass as bass
from concourse import mybir

ALU = mybir.AluOpType
ACT = mybir.ActivationFunctionType
AX = mybir.AxisListType
F32 = mybir.dt.float32
BF16 = mybir.dt.bfloat16
I32 = mybir.dt.int32

P = 128
EPS = 1e-5
NEG = -10000.0
K, V, Q = 0, 1, 2


def block_kernel(nc, x, ctx_in, mask, w_x, diag, w_in, b_in, w_out, b_out, g1, be1, g2, be2,
                 wg, w1, b1, w2, b2, out, xdisp):
    L, N, D = x.shape
    S2 = ctx_in.shape[1]
    E, _, FF = w1.shape
    NJ = N // P
    T = L * NJ
    DC = D // P
    FT = FF // P
    H = 4
    HD = D // H
    CAP = L * N // E
    PW = L * D
    DW = 2 * D + 2
    GATE, TOK = 2 * D, 2 * D + 1
    NTOK = 2 * L * N
    TA0 = NJ - 2
    assert L == 2 and NJ == E and DC == 2 and FT == 8 and NJ % 2 == 0 and CAP == 2 * P

    with ExitStack() as ctx:
        def sb(name, shape, dt=F32):
            return ctx.enter_context(nc.sbuf_tensor(name, shape, dt))

        def sem(name):
            return ctx.enter_context(nc.semaphore(name))

        def bank(name):
            return ctx.enter_context(nc.psum_tensor(name, [P, 512], F32))

        x_sb = sb("x_sb", [P, NJ * PW])
        disp = sb("disp", [P, T, DW])
        disp_lj = disp[:, :, :].rearrange("p (l j) w -> p j l w", l=L)
        xn = sb("xn", [P, PW])
        xnT = sb("xnT", [P, DC, L * P])
        x1T = sb("x1T", [P, DC, L * P])
        shifted = sb("shifted", [P, L, S2])
        probs = sb("probs", [P, L, S2])
        probsT = sb("probsT", [S2, L * P])
        xres = sb("xres", [P, PW])
        h_sb = sb("h_sb", [P, 2, PW])
        hb = sb("hb", [P, 2, PW])
        hT = sb("hT", [P, DC, L * P])
        hdT = sb("hdT", [P, DC, P])
        kvd = sb("kvd", [P, 2 * D])
        qb = sb("qb", [P, PW])
        v1b = sb("v1b", [P, D])
        prod = sb("prod", [P, PW])
        o_sb = sb("o_sb", [P, PW])
        oT = sb("oT", [P, DC, L * P])
        r_sb = sb("r_sb", [P, PW])
        rg = sb("rg", [P, PW])
        y1 = sb("y1", [P, 2, PW])
        y1T = sb("y1T", [P, DC, L * P])
        st = {n: sb(f"stats_{n}", [P, L, 6]) for n in "xhybz"}
        mv = {n: sb(f"mv_{n}", [P, L, 2]) for n in "xhyb"}
        zn = sb("zn", [P, PW])
        zw = sb("zw", [P, PW])
        mvz, rsz, nmr = sb("mv_z_all", [P, E, 2, 2]), sb("rstd_z_all", [P, E, 2]), sb("minus_mean_rstd", [P, E, 2])
        ve = {n: sb(f"vareps_{n}", [P, L]) for n in "xhybz"}
        rs = {n: sb(f"rstd_{n}", [P, L]) for n in "xhyb"}
        counts = sb("counts", [P, L])
        nmax = sb("nmax", [P, L])
        esum = sb("esum", [P, L])
        rsum = sb("rsum", [P, L])
        dsc = sb("dsc", [P, L * H])
        dm = sb("dm", [P, 2, L * H])
        pe2 = sb("pe2", [P, 2, L * H])
        psum2 = sb("psum2", [P, L * H])
        prec = sb("prec", [P, L * H])
        pr = sb("pr", [P, L * H])
        logits = sb("logits", [P, L, NJ, E])
        gmax = sb("gmax", [P, T])
        gsh = sb("gsh", [P, T, E])
        gex = sb("gex", [P, T, E])
        gsum = sb("gsum", [P, T])
        tokrow = sb("tokrow", [P, T])
        toki = sb("toki", [P, E, 2], I32)
        ismax = sb("ismax", [P, T, E])
        first = sb("first", [P, T])
        hot = sb("hot", [P, T, E], BF16)
        rank = posh = sb("rank_or_place", [P, T, E])
        loc = sb("loc", [P, T])
        over = sb("over", [P, T])
        slotf = sb("slotf", [P, T])
        slot = sb("slot", [P, T], I32)
        raw = sb("raw", [P, 5 * DC, D])
        w_raw, win_raw, wo_raw = raw[:, 0:DC, :], raw[:, DC:4 * DC, :], raw[:, 4 * DC:5 * DC, :]
        wT = sb("wT", [P, DC, D])
        winT = sb("winT", [P, DC, 3 * D])
        woT = sb("woT", [P, DC, D])
        ctx_sb = sb("ctx_sb", [S2, L, D])
        ctxT = sb("ctxT", [P, DC, L * S2])
        x2n = sb("x2n", [P, DC, L * S2])
        mask_i = sb("mask_i", [P, L * S2], I32)
        nmask = sb("nmask", [P, L, S2])
        diag_sb = sb("diag_sb", [DC, P])
        ndcol = sb("ndcol", [P, DC])
        wg_sb = sb("wg_sb", [P, DC, E])
        b1_sb = sb("b1_sb", [E, FF])
        b1T = sb("b1T", [P, FT, E])
        slots = sb("slots", [P, E, 2, DW])
        slots_f = slots[:, :, :, :].rearrange("p e s w -> p (e s w)")
        WW = 2 * DC * FF
        w1_sb = slots_f[:, 0:WW].rearrange("p (b c f) -> p b c f", b=2, c=DC)
        w2_sb = slots_f[:, WW:2 * WW].rearrange("p (b t d) -> p b t d", b=2, t=FT)
        w1T = sb("w1T", [P, FT, D])
        w12 = sb("w12", [P, E * DC * D])
        b12t = sb("b12t", [P, D])
        b12p = sb("b12p", [P, E * D])
        rows = {n: sb(f"row_{n}", [P, D]) for n in ("bq", "bv", "bo", "g1", "be1", "g2", "be2")}
        ident = sb("ident", [P, P])
        ones = sb("ones", [P, P])
        onesb = sb("onesb", [P, P], BF16)
        before = sb("before", [P, P], BF16)
        rev = sb("rev", [P, E])
        epst = sb("epst", [P, L])
        mhalf = sb("mhalf", [P, L])
        zero = disp[:, T - 2:T, :].rearrange("p t w -> p (t w)")
        xeT = w1T[:, :, :].rearrange("p (b c) n -> p b c n", b=4)
        base = x_sb
        disp_f = disp[:, :, :].rearrange("p t w -> p (t w)")
        zo, zt = disp_f[:, 0:NJ * PW], disp_f[:, NJ * PW:2 * NJ * PW]

        TA, TB, WA, WB, AC, BQ, BV, BK = [bank(n) for n in
                                          ("tpA", "tpB", "w1tA", "w1tB", "w12acc", "psQ", "psVQ", "psKV")]

        xeT_banks, ye_banks = (TA, TB, AC), (BV, BK, BQ)

        s_xl0, s_xl1, s_xlr = sem("x0_loaded"), sem("x1_loaded"), sem("xrest_loaded")
        s_wx, s_ctx, s_win, s_wo = sem("wx_loaded"), sem("ctx_loaded"), sem("win_loaded"), sem("wo_loaded")
        s_small, s_rows, s_b2 = sem("small_loaded"), sem("rows_loaded"), sem("b2_loaded")
        s_w1 = [sem("w1_loaded0"), sem("w1_loaded1")]
        s_w2 = [sem("w2_loaded0"), sem("w2_loaded1")]
        s_const, s_ident0, s_ident, s_tri, s_zero = sem("const_ready"), sem("ident_zeroed"), sem("ident_ready"), sem("tri_ready"), sem("zero_ready")
        s_wxT, s_woT, s_winT, s_ctxT, s_b1T = [sem(n) for n in ("wxT_psum", "woT_psum", "winT_psum", "ctxT_psum", "b1T_psum")]
        s_setT = sem("setup_transposes_copied")
        s_x2, s_x2n, s_dn, s_nm = sem("x2rep_psum"), sem("x2n_ready"), sem("b1T_ready"), sem("nmask_step")
        s_xn, s_xnTp, s_xnT = sem("xn_ready"), sem("xnT_psum"), sem("xnT_copied")
        s_x1p, s_x1 = sem("x1rep_psum"), sem("x1rep_ready")
        s_scp, s_shift, s_probs = sem("scores_psum"), sem("shifted_ready"), sem("probs_ready")
        s_prTp, s_prT, s_attp, s_xres = sem("probsT_psum"), sem("probsT_copied"), sem("attended_psum"), sem("xres_ready")
        s_h, s_hTp, s_hT, s_hd = sem("h_ready"), sem("hT_psum"), sem("hT_copied"), sem("hdiffT_ready")
        s_qp, s_kp, s_kvd, s_qv = sem("q_v_psum"), sem("k_v_diff_psum"), sem("k_v_diff_copied"), sem("q_v_biased")
        s_pd, s_pe2, s_o = sem("score_diff_ready"), sem("pair_exp_ready"), sem("o_ready")
        s_oTp, s_oT, s_prp = sem("oT_psum"), sem("oT_copied"), sem("projected_psum")
        s_r, s_y1 = sem("r_ready"), sem("y1_ready")
        s_y1Tp, s_y1T, s_lgp, s_lg = sem("y1T_psum"), sem("y1T_copied"), sem("logits_psum"), sem("logits_copied")
        s_wTp, s_wT = sem("w1T_psum"), sem("w1T_copied")
        s_w12p, s_w12, s_bp, s_b12 = sem("w12_psum"), sem("w12_copied"), sem("b12_step"), sem("b12_accumulated")
        s_hb, s_xb, s_y1c = sem("hb_ready"), sem("xb_ready"), sem("y1_kept")
        s_ln = {n: sem(f"ln_{n}_step") for n in "xhybz"}
        s_var = {n: sem(f"var_{n}_ready") for n in "xhybz"}
        s_ve = {n: sem(f"vareps_{n}_ready") for n in "xhybz"}
        s_rs = {n: sem(f"rstd_{n}_ready") for n in "xhybz"}
        s_att = sem("attention_step")
        s_g, s_gsh, s_gex, s_hot, s_pos = sem("router_step"), sem("gate_shifted"), sem("gate_exp"), sem("onehot_ready"), sem("positions_psum")
        s_slot = sem("slots_ready")
        s_zn, s_zw, s_based, s_bst = [sem(n) for n in ("zn_ready", "zw_ready", "base_ready", "base_stored")]
        s_zd, s_scat, s_xe = sem("dispatch_zeroed"), [sem("first_tiles_scattered"), sem("last_tiles_scattered")], [sem(f"xe_loaded{e}") for e in range(E)]
        s_xeTp, s_xeT, s_yep, s_ye = sem("xeT_psum"), sem("xeT_copied"), sem("ye_psum"), sem("ye_ready")
        s_z, s_nmr, s_zh, s_zg, s_zo, s_out = sem("z_step"), sem("nmr_ready"), sem("z_normed"), sem("zg_ready"), sem("out_rows_ready"), sem("out_stored")

        x_t = x.rearrange("l (j p) d -> p l j d", p=P)
        x_v = x_sb[:, :].rearrange("p (j l d) -> p l j d", l=L, d=D)
        xe_rows = xdisp.rearrange("(e s p) d -> p e s d", s=2, p=P)
        out_rows = out.rearrange("l n d -> (l n) d")

        block = ctx.enter_context(nc.Block())

        def pair(t, j):
            return t[:, bass.ds(j * PW, PW)].rearrange("p (l d) -> p l d", l=L)

        def both(t):
            return t.rearrange("p (l d) -> p l d", l=L)

        @block.sync
        def _(sp):
            for l in range(L):
                sp.dma_start(x_v[:, l, 0:1, :], x_t[:, l, 0:1, :]).then_inc(s_xl0, 16)
            sp.dma_start(w_raw[:, :, :], w_x.rearrange("(c p) d -> p c d", p=P)).then_inc(s_wx, 16)
            sp.dma_start(ctx_sb[:, :, :], ctx_in.rearrange("l s d -> s l d")).then_inc(s_ctx, 16)
            for l in range(L):
                sp.dma_start(x_v[:, l, 1:2, :], x_t[:, l, 1:2, :]).then_inc(s_xl1, 16)
            sp.dma_start(win_raw[:, :, :], w_in.rearrange("(c p) d -> p c d", p=P)).then_inc(s_win, 16)
            sp.dma_start(wo_raw[:, :, :], w_out.rearrange("(c p) d -> p c d", p=P)).then_inc(s_wo, 16)
            sp.dma_start(w1_sb[:, 0, :, :], w1[0].rearrange("(c p) f -> p c f", p=P)).then_inc(s_w1[0], 16)
            sp.dma_start(w2_sb[:, 0, :, :], w2[0].rearrange("(t p) d -> p t d", p=P)).then_inc(s_w2[0], 16)
            for n, v in (("bq", b_in[0:D]), ("bv", b_in[2 * D:3 * D]), ("bo", b_out), ("g1", g1), ("be1", be1), ("g2", g2), ("be2", be2)):
                sp.dma_start(rows[n][:, :], v.partition_broadcast(P)).then_inc(s_rows, 16)
            for l in range(L):
                sp.dma_start(x_v[:, l, 2:NJ, :], x_t[:, l, 2:NJ, :]).then_inc(s_xlr, 16)
            sp.dma_start(w1_sb[:, 1, :, :], w1[1].rearrange("(c p) f -> p c f", p=P)).then_inc(s_w1[1], 16)
            sp.dma_start(w2_sb[:, 1, :, :], w2[1].rearrange("(t p) d -> p t d", p=P)).then_inc(s_w2[1], 16)
            sp.wait_ge(s_zero, 2)
            sp.dma_start(b12p[0:1, :], b2.rearrange("(a e) d -> a (e d)", a=1)).then_inc(s_b2, 16)
            for e in range(E):
                sp.dma_start(xdisp[e * CAP:(e + 1) * CAP].rearrange("(p r) d -> p (r d)", p=P), zero).then_inc(s_zd, 16)
            out_t = out.rearrange("l (j p) d -> p l j d", p=P)
            with sp.Fori(1, NJ // 2) as i:
                for par in range(2):
                    e = i * 2 + par
                    sp.wait_ge(s_w12p, e - 1)
                    sp.dma_start(w1_sb[:, par, :, :], w1[bass.ds(e, 1)].rearrange("e (c p) f -> p (e c) f", p=P)).then_inc(s_w1[par], 16)
                    sp.wait_ge(s_b12, e - 1)
                    sp.dma_start(w2_sb[:, par, :, :], w2[bass.ds(e, 1)].rearrange("e (t p) d -> p (e t) d", p=P)).then_inc(s_w2[par], 16)
                    sp.wait_ge(s_based, e - 1)
                    sp.dma_start(out_t[:, :, bass.ds(e - 2, 1), :].rearrange("p l j d -> p (l j) d"), pair(base, e - 2)).then_inc(s_bst, 16)
            sp.wait_ge(s_based, NJ - 1)
            sp.dma_start(out_t[:, :, NJ - 2], pair(base, NJ - 2)).then_inc(s_bst, 16)
            sp.wait_ge(s_scat[0], 16 * (T - 2))
            sp.wait_ge(s_scat[1], 16 * 2)
            sp.wait_ge(s_w12p, E)
            sp.wait_ge(s_b12, E)
            for e in range(E):
                sp.dma_start(slots[:, e, :, :], xe_rows[:, e]).then_inc(s_xe[e], 16)
            sp.wait_ge(s_based, NJ)
            sp.dma_start(out_t[:, :, NJ - 1], pair(base, NJ - 1)).then_inc(s_bst, 16)
            sp.wait_ge(s_out, 16 * 2 * E)

        @block.gpsimd
        def _(pool):
            pool.memset(ident[:, :], 0.0).then_inc(s_ident0, 1)
            pool.wait_ge(s_ident0, 1)
            pool.affine_select(out=ident[:, :], in_=ident[:, :], compare_op=ALU.not_equal, fill=1.0, base=0,
                               pattern=[[-1, P]], channel_multiplier=1).then_inc(s_ident, 1)
            pool.memset(epst[:, :], EPS).then_inc(s_const, 1)
            pool.memset(mhalf[:, :], -0.5).then_inc(s_const, 1)
            pool.wait_ge(s_const, 2)

            def rstd(n, j):
                pool.wait_ge(s_var[n], j + 1)
                if n == "z" and j:
                    pool.wait_ge(s_rs[n], j)
                var, dst = (mvz[:, j, :, 1], rsz[:, j, :]) if n == "z" else (mv[n][:, :, 1], rs[n][:, :])
                pool.tensor_tensor(ve[n][:, :], var, epst[:, :], ALU.add).then_inc(s_ve[n], 1)
                pool.wait_ge(s_ve[n], j + 1)
                pool.tensor_tensor(dst, ve[n][:, :], mhalf[:, :], ALU.pow).then_inc(s_rs[n], 1)

            def constants():
                pool.memset(b12p[:, :], 0.0).then_inc(s_zero, 1)
                pool.memset(zero, 0.0).then_inc(s_zero, 1)
                pool.memset(ones[:, :], 1.0).then_inc(s_const, 1)
                pool.memset(onesb[:, :], 1.0).then_inc(s_zw, 1)
                pool.memset(before[:, :], 1.0).then_inc(s_tri, 1)
                pool.wait_ge(s_tri, 1)
                pool.affine_select(out=before[:, :], in_=before[:, :], compare_op=ALU.is_gt, fill=0.0, base=0,
                                   pattern=[[1, P]], channel_multiplier=-1).then_inc(s_const, 1)
                for e in range(E):
                    pool.memset(rev[:, e:e + 1], float(E - e)).then_inc(s_const, 1)
                for t in range(T):
                    pool.memset(tokrow[:, t:t + 1], float(t * P - NTOK)).then_inc(s_const, 1)

            def scatter(t):
                pool.indirect_dma_start(out=xdisp, out_offset=bass.IndirectOffsetOnAxis(ap=slot[:, t:t + 1], axis=0),
                                        in_=disp[:, t, :], in_offset=None,
                                        bounds_check=E * CAP - 1, oob_is_err=False).then_inc(s_scat[t >= T - 2], 16)

            def without_expert(j):
                pool.wait_ge(s_zn, j - 1)
                pool.tensor_tensor(both(zw[:, :]), both(zn[:, :]), rows["g2"][:, :].unsqueeze(1).broadcast_to([P, L, D]), ALU.mult).then_inc(s_zw, 1)
                pool.wait_ge(s_zw, j)
                pool.tensor_tensor(pair(base, j - 2), both(zw[:, :]),
                                   disp_lj[:, bass.ds(j - 2, 1), :, D:2 * D].rearrange("p j l d -> p (j l) d"), ALU.add).then_inc(s_based, 1)

            def step(j, par, cross, proj, ahead):
                if ahead:
                    rstd("x", j + 1)
                if proj:
                    rstd("y", j - 2)
                    rstd("b", j - 2)
                if cross:
                    rstd("h", j)
                    pool.wait_ge(s_xres, j * L + L)
                    pool.tensor_tensor(disp_lj[:, bass.ds(j, 1), :, D:2 * D].rearrange("p j l d -> p (j l) d"), both(xres[:, :]),
                                       rows["be2"][:, :].unsqueeze(1).broadcast_to([P, L, D]), ALU.add).then_inc(s_xb, 1)
                    pool.wait_ge(s_h, j + 1)
                    pool.tensor_tensor(both(hb[:, par, :]), both(h_sb[:, par % 2, :]), rows["bo"][:, :].unsqueeze(1).broadcast_to([P, L, D]), ALU.add).then_inc(s_hb, 1)
                if proj:
                    without_expert(j)

            rstd("x", 0)
            constants()
            pool.wait_ge(s_rows, 16 * 7)
            step(0, 0, True, False, True)
            step(1, 1, True, False, True)
            with pool.Fori(1, NJ // 2 - 1) as i:
                for par in range(2):
                    step(i * 2 + par, par, True, True, True)
            pool.wait_ge(s_zd, 16 * E)
            step(NJ - 2, 0, True, True, True)
            step(NJ - 1, 1, True, True, False)
            pool.wait_ge(s_y1c, NJ - 2)
            pool.wait_ge(s_slot, 1)
            for t in range(TA0):
                scatter(t)
            rstd("y", NJ - 2)
            rstd("y", NJ - 1)
            rstd("b", NJ - 2)
            without_expert(NJ)
            rstd("b", NJ - 1)
            pool.wait_ge(s_y1c, NJ)
            pool.wait_ge(s_slot, 2)
            for t in range(TA0, T):
                scatter(t)
            without_expert(NJ + 1)
            rstd("z", 0)
            for e in range(E):
                if e + 1 < E:
                    rstd("z", e + 1)
                pool.wait_ge(s_zo, e + 1)
                if e == 0:
                    pool.wait_ge(s_bst, 16 * NJ)
                for s in range(2):
                    c = (e * 2 + s) * D
                    pool.indirect_dma_start(out=out_rows, out_offset=bass.IndirectOffsetOnAxis(ap=toki[:, e, s:s + 1], axis=0),
                                            in_=zo[:, c:c + D], in_offset=None,
                                            bounds_check=L * N - 1, oob_is_err=False).then_inc(s_out, 16)

        @block.scalar
        def _(act):
            act.dma_start(mask_i[:, :], mask.rearrange("l s -> (l s)").partition_broadcast(P)).then_inc(s_small, 16)
            act.dma_start(diag_sb[:, :], diag.rearrange("(c p) -> c p", p=P)).then_inc(s_small, 16)
            act.dma_start(wg_sb[:, :, :], wg.rearrange("(c p) e -> p c e", p=P)).then_inc(s_small, 16)
            act.dma_start(b1_sb[:, :], b1).then_inc(s_small, 16)

            def copy(dst, src, done):
                act.activation(dst, src, ACT.Copy).then_inc(done, 1)

            act.wait_ge(s_wxT, 1)
            copy(wT[:, :, :].rearrange("p c h -> p (c h)"), TB[:, :], s_setT)
            act.wait_ge(s_ctxT, 1)
            copy(ctxT[:, :, :].rearrange("p c s -> p (c s)"), WA[:, 0:DC * L * S2], s_setT)
            act.wait_ge(s_b1T, 1)
            copy(b1T[:, :, :].rearrange("p t e -> p (t e)"), AC[:, 0:FT * E], s_dn)
            act.activation(ndcol[:, :], AC[:, FT * E:FT * E + DC], ACT.Copy, scale=-1.0).then_inc(s_w12, 1)
            act.wait_ge(s_winT, 3)
            for n, b in enumerate((BQ, BV, BK)):
                copy(winT[:, :, n * D:(n + 1) * D], b[:, :].rearrange("p (c o) -> p c o", c=DC), (s_wT, s_setT, s_lg)[n])
            act.wait_ge(s_woT, 1)
            copy(woT[:, :, :].rearrange("p c o -> p (c o)"), TA[:, :], s_y1T)

            def w1T_copy(j, k):
                act.wait_ge(s_wTp, j * 4 + (k + 1))
                b = (WA, WB)[k % 2]
                copy(w1T[:, 2 * k:2 * k + 2, :].rearrange("p t d -> p (t d)"), b[:, :], s_wT)

            def w12_copy(e):
                act.wait_ge(s_w12p, e + 1)
                copy(w12[:, bass.ds(e * (DC * D), DC * D)], AC[:, :], s_w12)

            def gates(n, a, b):
                act.wait_ge(s_gsh, n)
                act.activation(gex[:, a:b, :], gsh[:, a:b, :], ACT.Exp).then_inc(s_gex, 1)

            def hT_copy(j):
                act.wait_ge(s_hTp, j)
                copy(hT[:, :, :].rearrange("p c n -> p (c n)"), TA[:, :], s_hT)

            def oT_copy(j, b=TA):
                act.wait_ge(s_oTp, j - 1)
                copy(oT[:, :, :].rearrange("p c n -> p (c n)"), b[:, :], s_oT)

            def kvd_copy(j):
                act.wait_ge(s_kp, j)
                copy(kvd[:, :], BK[:, :], s_kvd)

            def pair_exp(j):
                act.wait_ge(s_pd, j)
                act.activation(pe2[:, :, :], dm[:, :, :], ACT.Exp, scale=HD ** -0.5).then_inc(s_pe2, 1)

            def y1_copies(j, par):
                act.wait_ge(s_y1Tp, j - 1)
                copy(y1T[:, :, :].rearrange("p c n -> p (c n)"), TA[:, :], s_y1T)
                copy(disp_lj[:, bass.ds(j - 2, 1), :, 0:D].rearrange("p j l d -> p (j l) d"), both(y1[:, par, :]), s_y1c)

            def xnT_copy(j):
                act.wait_ge(s_xnTp, j + 1)
                copy(xnT[:, :, :].rearrange("p c n -> p (c n)"), TB[:, :], s_xnT)

            def x1T_relu(j):
                act.wait_ge(s_x1p, j + 1)
                act.activation(x1T[:, :, :].rearrange("p c n -> p (c n)"), TB[:, :], ACT.Relu).then_inc(s_x1, 1)

            def scores_exp(j):
                act.wait_ge(s_shift, j + 1)
                for l in range(L):
                    last = act.activation(probs[:, l, :], shifted[:, l, :], ACT.Exp, scale=-1.0,
                                          bias=nmax[:, l:l + 1], accum_out=esum[:, l:l + 1])
                last.then_inc(s_probs, 1)

            def probsT_copy(j):
                act.wait_ge(s_prTp, j + 1)
                copy(probsT[:, :], TB[0:S2, 256:512], s_prT)

            xnT_copy(0)
            w1T_copy(0, 0)
            x1T_relu(0)
            w1T_copy(0, 1)
            scores_exp(0)
            probsT_copy(0)
            w1T_copy(0, 2)
            w1T_copy(0, 3)
            xnT_copy(1)
            x1T_relu(1)
            hT_copy(1)
            scores_exp(1)
            probsT_copy(1)
            kvd_copy(1)
            w12_copy(0)
            with act.Fori(1, NJ // 2) as i:
                for par in range(2):
                    j = i * 2 + par
                    w1T_copy(j - 1, 0)
                    pair_exp(j - 1)
                    w1T_copy(j - 1, 1)
                    xnT_copy(j)
                    hT_copy(j)
                    oT_copy(j)
                    x1T_relu(j)
                    kvd_copy(j)
                    w1T_copy(j - 1, 2)
                    w1T_copy(j - 1, 3)
                    scores_exp(j)
                    probsT_copy(j)
                    y1_copies(j, par)
                    w12_copy(j - 1)
            w1T_copy(E - 1, 0)
            pair_exp(NJ - 1)
            w1T_copy(E - 1, 1)
            hT_copy(NJ)
            gates(1, 0, TA0)
            kvd_copy(NJ)
            oT_copy(NJ)
            w1T_copy(E - 1, 2)
            pair_exp(NJ)
            w1T_copy(E - 1, 3)
            oT_copy(NJ + 1, BQ)
            y1_copies(NJ, 0)
            w12_copy(E - 1)
            y1_copies(NJ + 1, 1)
            gates(2, TA0, T)
            def z_norm(e):
                act.wait_ge(s_nmr, e + 1)
                for s in range(2):
                    c = (e * 2 + s) * D
                    last = act.activation(zo[:, c:c + D], zt[:, c:c + D], ACT.Identity, scale=rsz[:, e, s:s + 1], bias=nmr[:, e, s:s + 1])
                last.then_inc(s_zh, 1)

            for e in range(E + 3):
                if e < E:
                    act.wait_ge(s_xeTp, e + 1)
                    copy(xeT[:, e % 4, :, :].rearrange("p c n -> p (c n)"), xeT_banks[e % 3][:, :], s_xeT)
                if e >= 3:
                    z_norm(e - 3)

        @block.vector
        def _(dve):
            def norm_stats(n, src, j, steps, at, rstd=True):
                for l in range(L):
                    dve.bn_stats(st[n][:, l, :], src[:, l, :]).then_inc(s_ln[n], 1)
                dve.wait_ge(s_ln[n], j * steps + (at + L))
                dve.tensor_copy(counts[:, :], st[n][:, :, 0])
                for l in range(L):
                    last = dve.bn_aggr(mv[n][:, l, :], st[n][:, l, :])
                last.then_inc(s_var[n], 1)
                if rstd:
                    dve.wait_ge(s_rs[n], j + 1)

            def normed(n, dst, src, l):
                return dve.tensor_scalar(dst, src, mv[n][:, l, 0:1], rs[n][:, l:l + 1], ALU.subtract, ALU.mult)

            def cross_in(j):
                norm_stats("x", pair(x_sb, j), j, 2, 0)
                for l in range(L):
                    last = normed("x", xn[:, l * D:(l + 1) * D], x_sb[:, bass.ds(j * PW + l * D, D)], l)
                last.then_inc(s_xn, 1)

            def scores_shift(j):
                dve.wait_ge(s_nm, 1)
                dve.wait_ge(s_scp, j + 1)
                for l in range(L):
                    last = dve.tensor_tensor_reduce(out=shifted[:, l, :], in0=TB[:, l * S2:(l + 1) * S2], in1=nmask[:, l, :],
                                                    scale=1.0, scalar=3.0e38, op0=ALU.add, op1=ALU.min, accum_out=nmax[:, l:l + 1])
                last.then_inc(s_shift, 1)

            def cross_a(j):
                dve.wait_ge(s_probs, j + 1)
                dve.reciprocal(rsum[:, :], esum[:, :]).then_inc(s_ln["h"], 1)
                dve.wait_ge(s_attp, j + 1)
                if not isinstance(j, int) or j > 0:
                    dve.wait_ge(s_xb, j)
                dve.wait_ge(s_ln["h"], j * 3 + 1)
                for l in range(L):
                    dve.scalar_tensor_tensor(xres[:, l * D:(l + 1) * D], TB[:, l * D:(l + 1) * D], rsum[:, l:l + 1],
                                             x_sb[:, bass.ds(j * PW + l * D, D)], ALU.mult, ALU.add).then_inc(s_xres, 1)
                dve.wait_ge(s_xres, j * L + L)
                norm_stats("h", both(xres[:, :]), j, 3, 1, False)

            def cross_b(j, par):
                dve.wait_ge(s_rs["h"], j + 1)
                if not isinstance(j, int) or j > 1:
                    dve.wait_ge(s_hb, j - 1)
                for l in range(L):
                    last = normed("h", h_sb[:, par, l * D:(l + 1) * D], xres[:, l * D:(l + 1) * D], l)
                last.then_inc(s_h, 1)

            def diff(j):
                dve.wait_ge(s_hT, j)
                dve.tensor_tensor(hdT[:, :, :], hT[:, :, 0:P], hT[:, :, P:2 * P], ALU.subtract).then_inc(s_hd, 1)

            NATT = 10

            def attention_bias(j):
                dve.wait_ge(s_qp, j)
                dve.tensor_tensor(qb[:, 0:D], BQ[:, 0:D], rows["bq"][:, :], ALU.add).then_inc(s_att, 1)
                dve.tensor_tensor(qb[:, D:2 * D], BV[:, D:2 * D], rows["bq"][:, :], ALU.add).then_inc(s_att, 1)
                dve.tensor_tensor(v1b[:, :], BV[:, 0:D], rows["bv"][:, :], ALU.add).then_inc(s_qv, 1)

            def attention_a(j):
                base = (j - 1) * NATT
                dve.wait_ge(s_kvd, j)
                dve.wait_ge(s_att, base + 2)
                dve.tensor_tensor(both(prod[:, :]), both(qb[:, :]), kvd[:, 0:D].unsqueeze(1).broadcast_to([P, L, D]), ALU.mult).then_inc(s_att, 1)
                dve.wait_ge(s_att, base + 3)
                dve.tensor_reduce(dsc[:, :], prod[:, :].rearrange("p (g d) -> p g d", d=HD), AX.X, ALU.add).then_inc(s_att, 1)
                dve.wait_ge(s_att, base + 4)
                dve.tensor_scalar(dm[:, 0, :], dsc[:, :], 0.0, None, ALU.min).then_inc(s_att, 1)
                dve.tensor_scalar(dm[:, 1, :], dsc[:, :], -1.0, 0.0, ALU.mult, ALU.min).then_inc(s_pd, 1)

            def attention_b(j):
                base = (j - 1) * NATT
                dve.wait_ge(s_pe2, j)
                dve.tensor_tensor(psum2[:, :], pe2[:, 0, :], pe2[:, 1, :], ALU.add).then_inc(s_att, 1)
                dve.wait_ge(s_att, base + 6)
                dve.reciprocal(prec[:, :], psum2[:, :]).then_inc(s_att, 1)
                dve.wait_ge(s_att, base + 7)
                dve.tensor_tensor(pr[:, :], pe2[:, 0, :], prec[:, :], ALU.mult).then_inc(s_att, 1)
                dve.wait_ge(s_att, base + 8)
                for l in range(L):
                    dve.tensor_tensor(prod[:, l * D:(l + 1) * D].rearrange("p (h d) -> p h d", d=HD),
                                             kvd[:, D:2 * D].rearrange("p (h d) -> p h d", d=HD),
                                             pr[:, l * H:(l + 1) * H].unsqueeze(2).broadcast_to([P, H, HD]), ALU.mult).then_inc(s_att, 1)
                dve.wait_ge(s_att, base + 10)
                if not isinstance(j, int) or j > 1:
                    dve.wait_ge(s_oTp, j - 1)
                for l in range(L):
                    dve.tensor_tensor(o_sb[:, l * D:(l + 1) * D], prod[:, l * D:(l + 1) * D], v1b[:, :], ALU.add).then_inc(s_o, 1)

            def project_a(j, par, b=TA):
                dve.wait_ge(s_prp, j - 1)
                dve.wait_ge(s_hb, j - 1)
                dve.tensor_tensor(r_sb[:, :], b[:, :], hb[:, par, :], ALU.add).then_inc(s_r, 1)
                dve.wait_ge(s_r, j - 1)
                norm_stats("y", both(r_sb[:, :]), j - 2, 4, 0, False)

            def project_b(j, par):
                dve.wait_ge(s_var["y"], j - 1)
                for l in range(L):
                    dve.scalar_tensor_tensor(rg[:, l * D:(l + 1) * D], r_sb[:, l * D:(l + 1) * D], mv["y"][:, l, 0:1],
                                             rows["g1"][:, :], ALU.subtract, ALU.mult).then_inc(s_ln["y"], 1)
                dve.wait_ge(s_rs["y"], j - 1)
                dve.wait_ge(s_ln["y"], (j - 2) * 4 + 4)
                for l in range(L):
                    last = dve.scalar_tensor_tensor(y1[:, par, l * D:(l + 1) * D], rg[:, l * D:(l + 1) * D], rs["y"][:, l:l + 1],
                                                    rows["be1"][:, :], ALU.mult, ALU.add)
                last.then_inc(s_y1, 1)

            def base_stats(j, par):
                dve.wait_ge(s_y1, j - 1)
                norm_stats("b", both(y1[:, par, :]), j - 2, 2, 0, False)

            def base_norm(j, par):
                dve.wait_ge(s_rs["b"], j - 1)
                if not isinstance(j, int) or j > 2:
                    dve.wait_ge(s_zw, j - 1)
                for l in range(L):
                    last = normed("b", zn[:, l * D:(l + 1) * D], y1[:, par, l * D:(l + 1) * D], l)
                last.then_inc(s_zn, 1)

            def logits_copy(j):
                dve.wait_ge(s_lgp, j - 1)
                dve.tensor_copy(logits[:, :, bass.ds(j - 2, 1), :].rearrange("p l j e -> p (l j) e"),
                                BK[:, 0:L * E].rearrange("p (l e) -> p l e", l=L)).then_inc(s_lg, 1)

            def bias_sum(e, loaded, par):
                dve.wait_ge(s_w2[par], loaded)
                odd = b12p[:, bass.ds(e * D, D)]
                for k in range(FT):
                    acc = (b12t[:, :], odd)[k % 2]
                    if k == 0:
                        ins = dve.tensor_scalar(acc, w2_sb[:, par, k, :], b1T[:, k, bass.ds(e, 1)], None, ALU.mult)
                    else:
                        if k >= 2:
                            dve.wait_ge(s_bp, e * FT + (k - 1))
                        ins = dve.scalar_tensor_tensor(acc, w2_sb[:, par, k, :], b1T[:, k, bass.ds(e, 1)], acc, ALU.mult, ALU.add)
                    ins.then_inc(s_bp, 1)
                dve.wait_ge(s_bp, e * FT + FT)
                dve.tensor_tensor(odd, odd, b12t[:, :], ALU.add).then_inc(s_b12, 1)

            def step(j, loaded, par, last=False):
                diff(j)
                if not last:
                    dve.wait_ge(s_xnTp, j + 1)
                    cross_in(j + 1)
                bias_sum(j - 1, loaded, 1 - par)
                project_a(j, par)
                scores_shift(j)
                project_b(j, par)
                base_stats(j, par)
                attention_bias(j)
                cross_a(j)
                attention_a(j)
                cross_b(j, par)
                attention_b(j)
                base_norm(j, par)
                logits_copy(j)

            dve.wait_ge(s_xl0, 16 * L)
            cross_in(0)
            dve.wait_ge(s_small, 64)
            dve.tensor_scalar(nmask[:, :, :].rearrange("p l s -> p (l s)"), mask_i[:, :], 1.0, NEG, ALU.subtract, ALU.mult).then_inc(s_nm, 1)
            dve.wait_ge(s_w12, 1)
            dve.wait_ge(s_x2, 1)
            for c in range(DC):
                last = dve.tensor_scalar(x2n[:, c, :], WB[:, c * L * S2:(c + 1) * L * S2], 0.0, ndcol[:, c:c + 1], ALU.max, ALU.mult)
            last.then_inc(s_x2n, 1)
            dve.wait_ge(s_xl1, 16 * L)
            dve.wait_ge(s_xnTp, 1)
            cross_in(1)
            scores_shift(0)
            cross_a(0)
            cross_b(0, 0)
            dve.wait_ge(s_rows, 16 * 7)
            scores_shift(1)
            diff(1)
            dve.wait_ge(s_xlr, 16 * L)
            dve.wait_ge(s_xnTp, 2)
            cross_in(2)
            attention_bias(1)
            cross_a(1)
            attention_a(1)
            cross_b(1, 1)
            attention_b(1)
            dve.wait_ge(s_dn, 1)
            dve.wait_ge(s_b2, 16)
            bias_sum(0, 16, 0)
            with dve.Fori(1, NJ // 2 - 1) as i:
                for par in range(2):
                    step(i * 2 + par, i * 16 + par * 16, par)
            step(NJ - 2, (NJ // 2 - 1) * 16, 0)
            step(NJ - 1, NJ // 2 * 16, 1, True)

            n = [0]

            def then(ins):
                n[0] += 1
                ins.then_inc(s_g, 1)
                dve.wait_ge(s_g, n[0])

            def choose(k, a, b):
                lg = logits[:, :, :, :].rearrange("p l j e -> p (l j) e")[:, a:b, :]
                wide = lambda t: t.unsqueeze(2).broadcast_to([P, b - a, E])
                revb = rev[:, :].unsqueeze(1).broadcast_to([P, b - a, E])
                dve.wait_ge(s_lg, (NJ - 1, NJ + 1)[k - 1])
                then(dve.tensor_reduce(gmax[:, a:b], lg, AX.X, ALU.max))
                then(dve.tensor_tensor(ismax[:, a:b, :], lg, wide(gmax[:, a:b]), ALU.is_ge))
                dve.tensor_tensor(gsh[:, a:b, :], lg, wide(gmax[:, a:b]), ALU.subtract).then_inc(s_gsh, 1)
                then(dve.tensor_tensor(rank[:, a:b, :], ismax[:, a:b, :], revb, ALU.mult))
                then(dve.tensor_reduce(first[:, a:b], rank[:, a:b, :], AX.X, ALU.max))
                dve.tensor_tensor(hot[:, a:b, :], revb, wide(first[:, a:b]), ALU.is_equal).then_inc(s_hot, 1)

            def route(k, a, b):
                dve.wait_ge(s_hot, k)
                dve.wait_ge(s_gex, k)
                then(dve.tensor_reduce(gsum[:, a:b], gex[:, a:b, :], AX.X, ALU.add))
                then(dve.reciprocal(disp[:, a:b, GATE], gsum[:, a:b]))
                dve.wait_ge(s_pos, k)
                if k == 1:
                    then(dve.tensor_scalar(disp[:, :, TOK], tokrow[:, :], TB[:, T * E:T * E + 1], None, ALU.add))
                then(dve.tensor_tensor(posh[:, a:b, :], TB[:, a * E:b * E].rearrange("p (t e) -> p t e", e=E), hot[:, a:b, :], ALU.mult))
                then(dve.tensor_reduce(loc[:, a:b], posh[:, a:b, :], AX.X, ALU.add))
                dve.tensor_scalar(over[:, a:b], loc[:, a:b], float(CAP), float(2 * E * CAP), ALU.is_ge, ALU.mult).then_inc(s_g, 1)
                n[0] += 1
                then(dve.scalar_tensor_tensor(slotf[:, a:b], first[:, a:b], -float(CAP), loc[:, a:b], ALU.mult, ALU.add))
                dve.scalar_tensor_tensor(slot[:, a:b], slotf[:, a:b], float(E * CAP), over[:, a:b], ALU.add, ALU.add).then_inc(s_slot, 1)

            diff(NJ)
            dve.wait_ge(s_const, 2 + 2 + E + T)
            choose(1, 0, TA0)
            attention_bias(NJ)
            route(1, 0, TA0)
            attention_a(NJ)
            attention_b(NJ)
            project_a(NJ, 0)
            project_b(NJ, 0)
            project_a(NJ + 1, 1, BQ)
            base_stats(NJ, 0)
            logits_copy(NJ)
            project_b(NJ + 1, 1)
            base_norm(NJ, 0)
            base_stats(NJ + 1, 1)
            logits_copy(NJ + 1)
            choose(2, TA0, T)
            route(2, TA0, T)
            base_norm(NJ + 1, 1)
            bias_sum(E - 1, NJ // 2 * 16, 1)
            def expert_sum(e):
                dve.wait_ge(s_yep, e + 1)
                dve.tensor_scalar(toki[:, e, :], slots[:, e, :, TOK], float(NTOK), None, ALU.add).then_inc(s_z, 1)
                for s in range(2):
                    c = (e * 2 + s) * D
                    dve.scalar_tensor_tensor(zt[:, c:c + D], ye_banks[e % 3][:, s * D:(s + 1) * D], slots[:, e, s, GATE:GATE + 1],
                                             slots[:, e, s, 0:D], ALU.mult, ALU.add).then_inc(s_z, 1)
                dve.wait_ge(s_z, e * 3 + 3)
                for s in range(2):
                    c = (e * 2 + s) * D
                    dve.bn_stats(st["z"][:, s, :], zt[:, c:c + D]).then_inc(s_ln["z"], 1)
                dve.wait_ge(s_ln["z"], e * 2 + 2)
                for s in range(2):
                    last = dve.bn_aggr(mvz[:, e, s, :], st["z"][:, s, :])
                last.then_inc(s_var["z"], 1)

            def minus_mean_rstd(e):
                dve.wait_ge(s_var["z"], e + 1)
                dve.wait_ge(s_rs["z"], e + 1)
                dve.scalar_tensor_tensor(nmr[:, e, :], mvz[:, e, :, 0], -1.0, rsz[:, e, :], ALU.mult, ALU.mult).then_inc(s_nmr, 1)

            def expert_out(e):
                zs = both(zo[:, e * 2 * D:(e + 1) * 2 * D])
                dve.wait_ge(s_zh, e + 1)
                dve.tensor_tensor(zs, zs, rows["g2"][:, :].unsqueeze(1).broadcast_to([P, 2, D]), ALU.mult).then_inc(s_zg, 1)
                dve.wait_ge(s_zg, e + 1)
                dve.tensor_tensor(zs, zs, slots[:, e, :, D:2 * D], ALU.add).then_inc(s_zo, 1)

            dve.wait_ge(s_based, NJ)
            for e in range(E + 2):
                if e < E:
                    expert_sum(e)
                if e >= 2:
                    expert_out(e - 2)
                if 1 <= e <= E:
                    minus_mean_rstd(e - 1)

        @block.tensor
        def _(pe):
            pe.wait_ge(s_ident, 1)
            pe.wait_ge(s_wx, 16)
            for c in range(DC):
                for h in range(DC):
                    last = pe.transpose(TB[:, c * D + h * P:c * D + (h + 1) * P], w_raw[:, h, c * P:(c + 1) * P], ident[:, :])
            last.then_inc(s_wxT, 1)
            pe.wait_ge(s_ctx, 16)
            for c in range(DC):
                for l in range(L):
                    last = pe.transpose(WA[:, (c * L + l) * S2:(c * L + l + 1) * S2], ctx_sb[:, l, c * P:(c + 1) * P], ident[0:S2, 0:S2])
            last.then_inc(s_ctxT, 1)
            pe.wait_ge(s_small, 64)
            for t in range(FT):
                last = pe.transpose(AC[:, t * E:(t + 1) * E], b1_sb[:, t * P:(t + 1) * P], ident[0:E, 0:E])
            pe.transpose(AC[:, FT * E:FT * E + DC], diag_sb[:, :], ident[0:DC, 0:DC]).then_inc(s_b1T, 1)
            pe.wait_ge(s_setT, 2)
            for h in range(DC):
                for c in range(DC):
                    last = pe.matmul(WB[:, h * L * S2:(h + 1) * L * S2], wT[:, c, h * P:(h + 1) * P], ctxT[:, c, :], start=(c == 0), stop=(c == DC - 1))
            last.then_inc(s_x2, 1)
            pe.wait_ge(s_win, 16)
            for n, b in enumerate((BQ, BV, BK)):
                for c in range(DC):
                    for a in range(DC):
                        o = ((n + 1) % 3) * DC + a
                        last = pe.transpose(b[:, c * D + a * P:c * D + (a + 1) * P], win_raw[:, o, c * P:(c + 1) * P], ident[:, :])
                last.then_inc(s_winT, 1)
            pe.wait_ge(s_wo, 16)
            for c in range(DC):
                for a in range(DC):
                    last = pe.transpose(TA[:, c * D + a * P:c * D + (a + 1) * P], wo_raw[:, a, c * P:(c + 1) * P], ident[:, :])
            last.then_inc(s_woT, 1)
            pe.wait_ge(s_x2n, 1)
            pe.wait_ge(s_setT, 3)
            pe.wait_ge(s_wT, 1)
            pe.wait_ge(s_y1T, 1)
            pe.wait_ge(s_lg, 1)
            pe.wait_ge(s_dn, 1)
            pe.wait_ge(s_w12, 1)

            def w1_transpose(e, k, par):
                b = (WA, WB)[k % 2]
                pe.wait_ge(s_wT, e * 4 + (k if k >= 2 else 1))
                for a in range(2):
                    for c in range(DC):
                        last = pe.transpose(b[:, a * D + c * P:a * D + (c + 1) * P], w1_sb[:, par, c, (2 * k + a) * P:(2 * k + a + 1) * P], ident[:, :])
                last.then_inc(s_wTp, 1)

            def w12_part(c, t0, t1, par):
                for t in range(t0, t1):
                    last = pe.matmul(AC[:, c * D:(c + 1) * D], w1T[:, t, c * P:(c + 1) * P], w2_sb[:, par, t, :], start=(t == 0), stop=(t == FT - 1))
                return last

            def w12_begin(e, loaded, par):
                pe.wait_ge(s_w2[par], loaded)
                pe.wait_ge(s_w12, e + 1)
                pe.wait_ge(s_wT, e * 4 + 2)
                w12_part(0, 0, 2, par)

            def transposes(b, src):
                for c in range(DC):
                    for l in range(L):
                        last = pe.transpose(b[:, (c * L + l) * P:(c * L + l + 1) * P], src[:, l * D + c * P:l * D + (c + 1) * P], ident[:, :])
                return last

            def query_value(j):
                pe.wait_ge(s_hT, j)
                if not isinstance(j, int) or j > 1:
                    pe.wait_ge(s_qv, j - 1)
                for c in range(DC):
                    pe.matmul(BQ[:, 0:D], hT[:, c, 0:P], winT[:, c, Q * D:(Q + 1) * D], start=(c == 0), stop=(c == DC - 1))
                for c in range(DC):
                    last = pe.matmul(BV[:, :], hT[:, c, P:2 * P], winT[:, c, V * D:(Q + 1) * D], start=(c == 0), stop=(c == DC - 1))
                last.then_inc(s_qp, 1)

            def key_value_diff(j):
                pe.wait_ge(s_hd, j)
                if not isinstance(j, int) or j > 1:
                    pe.wait_ge(s_kvd, j - 1)
                    pe.wait_ge(s_lg, j - 1)
                for c in range(DC):
                    last = pe.matmul(BK[:, :], hdT[:, c, :], winT[:, c, K * D:(V + 1) * D], start=(c == 0), stop=(c == DC - 1))
                last.then_inc(s_kp, 1)

            def out_projection(j, b=TA):
                pe.wait_ge(s_oT, j - 1)
                for l in range(L):
                    for c in range(DC):
                        last = pe.matmul(b[:, l * D:(l + 1) * D], oT[:, c, l * P:(l + 1) * P], woT[:, c, :], start=(c == 0), stop=(c == DC - 1))
                last.then_inc(s_prp, 1)

            def y1_transposes(j, par):
                pe.wait_ge(s_y1, j - 1)
                transposes(TA, y1[:, par, :]).then_inc(s_y1Tp, 1)

            def router_logits(j):
                pe.wait_ge(s_y1T, j)
                for l in range(L):
                    for c in range(DC):
                        last = pe.matmul(BK[:, l * E:(l + 1) * E], y1T[:, c, l * P:(l + 1) * P], wg_sb[:, c, :], start=(c == 0), stop=(c == DC - 1))
                last.then_inc(s_lgp, 1)

            def xn_transposes(j):
                pe.wait_ge(s_xn, j + 1)
                if not isinstance(j, int) or j > 0:
                    pe.wait_ge(s_xres, j * L)
                transposes(TB, xn[:, :]).then_inc(s_xnTp, 1)

            def x1_rep(j):
                pe.wait_ge(s_xnT, j + 1)
                for h in range(DC):
                    for c in range(DC):
                        last = pe.matmul(TB[:, h * L * P:(h + 1) * L * P], wT[:, c, h * P:(h + 1) * P], xnT[:, c, :], start=(c == 0), stop=(c == DC - 1))
                last.then_inc(s_x1p, 1)

            def scores(j):
                pe.wait_ge(s_x1, j + 1)
                for l in range(L):
                    for c in range(DC):
                        last = pe.matmul(TB[:, l * S2:(l + 1) * S2], x1T[:, c, l * P:(l + 1) * P], x2n[:, c, l * S2:(l + 1) * S2], start=(c == 0), stop=(c == DC - 1))
                last.then_inc(s_scp, 1)

            def probs_transposes(j):
                pe.wait_ge(s_probs, j + 1)
                for l in range(L):
                    last = pe.transpose(TB[0:S2, 256 + l * P:256 + (l + 1) * P], probs[:, l, :], ident[:, :])
                last.then_inc(s_prTp, 1)

            def attended(j):
                pe.wait_ge(s_prT, j + 1)
                for l in range(L):
                    last = pe.matmul(TB[:, l * D:(l + 1) * D], probsT[:, l * P:(l + 1) * P], ctx_sb[:, l, :], start=True, stop=True)
                last.then_inc(s_attp, 1)

            def h_transposes(j, par):
                pe.wait_ge(s_h, j)
                if not isinstance(j, int) or j > 1:
                    pe.wait_ge(s_y1T, j - 1)
                transposes(TA, h_sb[:, 1 - par, :]).then_inc(s_hTp, 1)

            def o_transposes(j, b=TA):
                pe.wait_ge(s_o, j * L - L)
                transposes(b, o_sb[:, :]).then_inc(s_oTp, 1)

            def step(j, loaded, par):
                e = j - 1
                b = 1 - par
                pe.wait_ge(s_w1[b], loaded)
                w1_transpose(e, 0, b)
                w1_transpose(e, 1, b)
                xn_transposes(j)
                w12_begin(e, loaded, b)
                h_transposes(j, par)
                pe.wait_ge(s_wT, e * 4 + 3)
                w12_part(0, 2, 4, b)
                query_value(j)
                o_transposes(j)
                x1_rep(j)
                key_value_diff(j)
                out_projection(j)
                w1_transpose(e, 2, b)
                w1_transpose(e, 3, b)
                scores(j)
                pe.wait_ge(s_wT, e * 4 + 5)
                w12_part(0, 4, 8, b)
                probs_transposes(j)
                w12_part(1, 0, 4, b)
                attended(j)
                y1_transposes(j, par)
                w12_part(1, 4, 8, b).then_inc(s_w12p, 1)
                pe.wait_ge(s_kvd, j)
                router_logits(j)

            def places(k, a, b):
                pe.wait_ge(s_hot, k)
                if k == 1:
                    pe.wait_ge(s_xres, NJ * L)
                    pe.matmul(TB[:, T * E:T * E + 1], before[:, :], onesb[:, 0:1], start=True, stop=True)
                pe.matmul(TB[:, a * E:b * E], before[:, :], hot[:, a:b, :].rearrange("p t e -> p (t e)"), start=True, stop=False)
                for t in range(b - 1):
                    f = max(t + 1, a)
                    last = pe.matmul(TB[:, f * E:b * E].rearrange("p (t e) -> p t e", e=E), onesb[:, :],
                                     hot[:, t:t + 1, :].broadcast_to([P, b - f, E]), start=False, stop=(t == b - 2))
                last.then_inc(s_pos, 1)

            xn_transposes(0)
            pe.wait_ge(s_w1[0], 16)
            w1_transpose(0, 0, 0)
            x1_rep(0)
            w1_transpose(0, 1, 0)
            scores(0)
            w12_begin(0, 16, 0)
            probs_transposes(0)
            w1_transpose(0, 2, 0)
            attended(0)
            w1_transpose(0, 3, 0)
            w12_part(0, 2, 4, 0)
            xn_transposes(1)
            pe.wait_ge(s_wT, 5)
            w12_part(0, 4, 6, 0)
            x1_rep(1)
            w12_part(0, 6, 8, 0)
            h_transposes(1, 1)
            scores(1)
            query_value(1)
            key_value_diff(1)
            probs_transposes(1)
            w12_part(1, 0, 2, 0)
            attended(1)
            w12_part(1, 2, 8, 0).then_inc(s_w12p, 1)
            with pe.Fori(1, NJ // 2) as i:
                for par in range(2):
                    step(i * 2 + par, i * 16 + par * 16, par)

            pe.wait_ge(s_w1[1], NJ // 2 * 16)
            w1_transpose(E - 1, 0, 1)
            w1_transpose(E - 1, 1, 1)
            w12_begin(E - 1, NJ // 2 * 16, 1)
            h_transposes(NJ, 0)
            pe.wait_ge(s_wT, (E - 1) * 4 + 3)
            w12_part(0, 2, 4, 1)
            query_value(NJ)
            places(1, 0, TA0)
            key_value_diff(NJ)
            o_transposes(NJ)
            w1_transpose(E - 1, 2, 1)
            out_projection(NJ)
            w1_transpose(E - 1, 3, 1)
            pe.wait_ge(s_wT, E * 4 + 1)
            w12_part(0, 4, 6, 1)

            pe.wait_ge(s_qv, NJ)
            o_transposes(NJ + 1, BQ)
            w12_part(0, 6, 8, 1)
            out_projection(NJ + 1, BQ)
            y1_transposes(NJ, 0)
            w12_part(1, 0, 4, 1)
            pe.wait_ge(s_kvd, NJ)
            router_logits(NJ)
            w12_part(1, 4, 8, 1).then_inc(s_w12p, 1)
            y1_transposes(NJ + 1, 1)
            pe.wait_ge(s_lg, NJ)
            router_logits(NJ + 1)
            places(2, TA0, T)

            def bias(e):
                pe.matmul(ye_banks[e % 3][:, :].rearrange("p (s d) -> p s d", s=2), ones[:, :],
                          b12p[:, e * D:(e + 1) * D].unsqueeze(1).broadcast_to([P, 2, D]), start=True, stop=False)

            def slots_transposed(e):
                pe.wait_ge(s_xe[e], 16)
                if e >= 3:
                    pe.wait_ge(s_xeT, e - 2)
                for c in range(DC):
                    for s in range(2):
                        last = pe.transpose(xeT_banks[e % 3][:, (c * 2 + s) * P:(c * 2 + s + 1) * P],
                                            slots[:, e, s, c * P:(c + 1) * P], ident[:, :])
                last.then_inc(s_xeTp, 1)

            pe.wait_ge(s_slot, 2)
            pe.wait_ge(s_w12, E + 1)
            pe.wait_ge(s_lg, NJ + 1)
            pe.wait_ge(s_r, NJ)
            pe.wait_ge(s_b12, E)
            pe.wait_ge(s_scat[0], 16 * (T - 2))
            for e in range(3):
                bias(e)
            slots_transposed(0)
            slots_transposed(1)
            for e in range(E):
                for ahead in {0: (), 1: (2,), 2: (3, 4)}.get(e, (e + 2,)):
                    if ahead < E:
                        slots_transposed(ahead)
                pe.wait_ge(s_xeT, e + 1)
                if e >= 3:
                    pe.wait_ge(s_z, (e - 2) * 3)
                    bias(e)
                for s in range(2):
                    for c in range(DC):
                        last = pe.matmul(ye_banks[e % 3][:, s * D:(s + 1) * D], xeT[:, e % 4, c, s * P:(s + 1) * P],
                                         w12[:, (e * DC + c) * D:(e * DC + c + 1) * D], start=False, stop=(s == 1 and c == DC - 1))
                last.then_inc(s_yep, 1)


_INS = ["x", "ctx_1024", "mask_BxS2_if1", "L0_xattn_W", "L0_xattn_diagonal", "L0_ffn_in_proj_w", "L0_ffn_in_proj_b",
        "L0_ffn_out_proj_w", "L0_ffn_out_proj_b", "L0_ffn_ln1_g", "L0_ffn_ln1_b", "L0_ffn_ln2_g", "L0_ffn_ln2_b",
        "L0_ffn_wg", "L0_ffn_w1", "L0_ffn_b1", "L0_ffn_w2", "L0_ffn_b2"]


def kernel(**inputs):
    import numpy as np
    import concourse.bacc as bacc
    from concourse.bass_utils import run_bass_kernel_spmd as run

    nc = bacc.Bacc("TRN2", target_bir_lowering=False, num_devices=1)
    arrays, args = {}, []
    for name in _INS:
        a = np.ascontiguousarray(inputs[name])
        arrays["in_" + name] = a
        args.append(nc.dram_tensor("in_" + name, a.shape, mybir.dt.from_np(a.dtype), kind="ExternalInput").ap())
    shape = inputs["x"].shape
    args.append(nc.dram_tensor("out_x", shape, F32, kind="ExternalOutput").ap())
    args.append(nc.dram_tensor("slot_rows", [shape[0] * shape[1], 2 * shape[2] + 2], F32, kind="Internal").ap())
    block_kernel(nc, *args)
    r = run(nc, [arrays], core_ids=[0])
    return r.results[0]["out_x"]
```

```python
from contextlib import ExitStack

import concourse.bass as bass
from concourse import mybir

ALU = mybir.AluOpType
ACT = mybir.ActivationFunctionType
AX = mybir.AxisListType
F32 = mybir.dt.float32
BF16 = mybir.dt.bfloat16
I32 = mybir.dt.int32

P = 128
EPS = 1e-5
NEG = -10000.0
K, V, Q = 0, 1, 2


def block_kernel(nc, x, ctx_in, mask, w_x, diag, w_in, b_in, w_out, b_out, g1, be1, g2, be2,
                 wg, w1, b1, w2, b2, out, xdisp):
    L, N, D = x.shape
    S2 = ctx_in.shape[1]
    E, _, FF = w1.shape
    NJ = N // P
    T = L * NJ
    DC = D // P
    FT = FF // P
    H = 4
    HD = D // H
    CAP = L * N // E
    PW = L * D
    DW = 2 * D + 2
    GATE, TOK = 2 * D, 2 * D + 1
    NTOK = 2 * L * N
    EARLY = NJ - 2
    assert L == 2 and NJ == E and DC == 2 and FT == 8 and NJ % 2 == 0 and CAP == 2 * P

    with ExitStack() as ctx:
        def sb(name, shape, dt=F32):
            return ctx.enter_context(nc.sbuf_tensor(name, shape, dt))

        def sem(name):
            return ctx.enter_context(nc.semaphore(name))

        def bank(name):
            return ctx.enter_context(nc.psum_tensor(name, [P, 512], F32))

        x_sb = sb("x_sb", [P, NJ * PW])
        disp = sb("disp", [P, T, DW])
        disp_t = disp[:, :, :].rearrange("p (l j) w -> p l j w", l=L)
        disp_lj = disp[:, :, :].rearrange("p (l j) w -> p j l w", l=L)
        xn = sb("xn", [P, PW])
        xnT = sb("xnT", [P, DC, L * P])
        x1T = sb("x1T", [P, DC, L * P])
        shifted = sb("shifted", [P, L, S2])
        probs = sb("probs", [P, L, S2])
        probsT = sb("probsT", [S2, L * P])
        xres = sb("xres", [P, PW])
        h_sb = sb("h_sb", [P, 2, PW])
        hb = sb("hb", [P, 2, PW])
        hT = sb("hT", [P, DC, L * P])
        hdT = sb("hdT", [P, DC, P])
        kvd = sb("kvd", [P, 2 * D])
        qb = sb("qb", [P, PW])
        v1b = sb("v1b", [P, D])
        prod = sb("prod", [P, PW])
        o_sb = sb("o_sb", [P, PW])
        oT = sb("oT", [P, DC, L * P])
        r_sb = sb("r_sb", [P, PW])
        rg = sb("rg", [P, PW])
        y1 = sb("y1", [P, 2, PW])
        y1T = sb("y1T", [P, DC, L * P])
        st = {n: sb(f"stats_{n}", [P, L, 6]) for n in "xhybz"}
        mv = {n: sb(f"mv_{n}", [P, L, 2]) for n in "xhyb"}
        zn = sb("zn", [P, PW])
        zw = sb("zw", [P, PW])
        mvz, rsz, nmr = sb("mv_z_all", [P, E, 2, 2]), sb("rstd_z_all", [P, E, 2]), sb("minus_mean_rstd", [P, E, 2])
        ve = {n: sb(f"vareps_{n}", [P, L]) for n in "xhybz"}
        rs = {n: sb(f"rstd_{n}", [P, L]) for n in "xhyb"}
        counts = sb("counts", [P, L])
        nmax = sb("nmax", [P, L])
        esum = sb("esum", [P, L])
        rsum = sb("rsum", [P, L])
        dsc = sb("dsc", [P, L * H])
        dm = sb("dm", [P, 2, L * H])
        pe2 = sb("pe2", [P, 2, L * H])
        psum2 = sb("psum2", [P, L * H])
        prec = sb("prec", [P, L * H])
        pr = sb("pr", [P, L * H])
        logits = sb("logits", [P, L, NJ, E])
        gmax = sb("gmax", [P, L, NJ])
        gsh = sb("gsh", [P, L, NJ, E])
        gex = sb("gex", [P, L, NJ, E])
        gsum = sb("gsum", [P, L, NJ])
        tokrow = sb("tokrow", [P, T])
        toki = sb("toki", [P, E, 2], I32)
        first = sb("first", [P, L, NJ])
        hot = sb("hot", [P, 2, L, NJ, E], BF16)
        pick = sb("pick", [P, 2, L, NJ, E])
        ismax, rank = pick[:, 0], pick[:, 1]
        loc = sb("loc", [P, 2, L, NJ])
        sign = sb("sign", [P, L])
        over = sb("over", [P, L, NJ])
        slotf = sb("slotf", [P, L, NJ])
        slot = sb("slot", [P, L, NJ], I32)
        raw = sb("raw", [P, 5 * DC, D])
        w_raw, win_raw, wo_raw = raw[:, 0:DC, :], raw[:, DC:4 * DC, :], raw[:, 4 * DC:5 * DC, :]
        wT = sb("wT", [P, DC, D])
        winT = sb("winT", [P, DC, 3 * D])
        woT = sb("woT", [P, DC, D])
        ctx_sb = sb("ctx_sb", [S2, L, D])
        ctxT = sb("ctxT", [P, DC, L * S2])
        x2n = sb("x2n", [P, DC, L * S2])
        mask_i = sb("mask_i", [P, L * S2], I32)
        nmask = sb("nmask", [P, L, S2])
        diag_sb = sb("diag_sb", [DC, P])
        ndcol = sb("ndcol", [P, DC])
        wg_sb = sb("wg_sb", [P, DC, E])
        b1_sb = sb("b1_sb", [E, FF])
        b1T = sb("b1T", [P, FT, E])
        slots = sb("slots", [P, E, 2, DW])
        slots_f = slots[:, :, :, :].rearrange("p e s w -> p (e s w)")
        WW = 2 * DC * FF
        w1_sb = slots_f[:, 0:WW].rearrange("p (b c f) -> p b c f", b=2, c=DC)
        w2_sb = slots_f[:, WW:2 * WW].rearrange("p (b t d) -> p b t d", b=2, t=FT)
        w1T = sb("w1T", [P, FT, D])
        w12 = sb("w12", [P, E * DC * D])
        b12t = sb("b12t", [P, D])
        b12p = sb("b12p", [P, E * D])
        rows = {n: sb(f"row_{n}", [P, D]) for n in ("bq", "bv", "bo", "g1", "be1", "g2", "be2")}
        ident = sb("ident", [P, P])
        ones = sb("ones", [P, P])
        onesb = sb("onesb", [P, P], BF16)
        before = sb("before", [P, P], BF16)
        rev = sb("rev", [P, E])
        epst = sb("epst", [P, L])
        mhalf = sb("mhalf", [P, L])
        zero = disp[:, T - 2:T, :].rearrange("p t w -> p (t w)")
        xeT = w1T[:, :, :].rearrange("p (b c) n -> p b c n", b=4)
        base = x_sb
        disp_f = disp[:, :, :].rearrange("p t w -> p (t w)")
        zo, zt = disp_f[:, 0:NJ * PW], disp_f[:, NJ * PW:2 * NJ * PW]

        TA, TB, WA, WB, AC, BQ, BV, BK = [bank(n) for n in
                                          ("tpA", "tpB", "w1tA", "w1tB", "w12acc", "psQ", "psVQ", "psKV")]

        xeT_banks, ye_banks = (TA, TB, AC), (BV, BK, BQ, WA, WB)

        s_xl0, s_xl1, s_xlr = sem("x0_loaded"), sem("x1_loaded"), sem("xrest_loaded")
        s_wx, s_ctx, s_win, s_wo = sem("wx_loaded"), sem("ctx_loaded"), sem("win_loaded"), sem("wo_loaded")
        s_small, s_mask, s_rows, s_b2 = sem("diag_b1_loaded"), sem("mask_wg_loaded"), sem("rows_loaded"), sem("b2_loaded")
        s_w1 = [sem("w1_loaded0"), sem("w1_loaded1")]
        s_w2 = [sem("w2_loaded0"), sem("w2_loaded1")]
        s_const, s_ident0, s_ident, s_tri, s_zero = sem("const_ready"), sem("ident_zeroed"), sem("ident_ready"), sem("tri_ready"), sem("zero_ready")
        s_wxT, s_woT, s_winT, s_ctxT, s_b1T = [sem(n) for n in ("wxT_psum", "woT_psum", "winT_psum", "ctxT_psum", "b1T_psum")]
        s_setT = sem("setup_transposes_copied")
        s_x2, s_x2n, s_dn, s_nm = sem("x2rep_psum"), sem("x2n_ready"), sem("b1T_ready"), sem("nmask_step")
        s_xn, s_xnTp, s_xnT = sem("xn_ready"), sem("xnT_psum"), sem("xnT_copied")
        s_x1p, s_x1 = sem("x1rep_psum"), sem("x1rep_ready")
        s_scp, s_shift, s_probs = sem("scores_psum"), sem("shifted_ready"), sem("probs_ready")
        s_prTp, s_prT, s_attp, s_xres = sem("probsT_psum"), sem("probsT_copied"), sem("attended_psum"), sem("xres_ready")
        s_h, s_hTp, s_hT, s_hd = sem("h_ready"), sem("hT_psum"), sem("hT_copied"), sem("hdiffT_ready")
        s_qp, s_kp, s_kvd, s_qv = sem("q_v_psum"), sem("k_v_diff_psum"), sem("k_v_diff_copied"), sem("q_v_biased")
        s_pd, s_pe2, s_o = sem("score_diff_ready"), sem("pair_exp_ready"), sem("o_ready")
        s_oTp, s_oT, s_prp = sem("oT_psum"), sem("oT_copied"), sem("projected_psum")
        s_r, s_y1 = sem("r_ready"), sem("y1_ready")
        s_y1Tp, s_y1T, s_lgp, s_lg = sem("y1T_psum"), sem("y1T_copied"), sem("logits_psum"), sem("logits_copied")
        s_wTp, s_wT = sem("w1T_psum"), sem("w1T_copied")
        s_w12p, s_w12, s_bp, s_b12 = sem("w12_psum"), sem("w12_copied"), sem("b12_step"), sem("b12_accumulated")
        s_hb, s_xb, s_y1c = sem("hb_ready"), sem("xb_ready"), sem("y1_kept")
        s_ln = {n: sem(f"ln_{n}_step") for n in "xhybz"}
        s_var = {n: sem(f"var_{n}_ready") for n in "xhybz"}
        s_ve = {n: sem(f"vareps_{n}_ready") for n in "xhybz"}
        s_rs = {n: sem(f"rstd_{n}_ready") for n in "xhybz"}
        s_att = sem("attention_step")
        s_g, s_gsh, s_gex, s_hot, s_pos = sem("router_step"), sem("gate_shifted"), sem("gate_exp"), sem("onehot_ready"), sem("positions_psum")
        s_slot = sem("slots_ready")
        s_zn, s_zw, s_based, s_bst = [sem(n) for n in ("zn_ready", "zw_ready", "base_ready", "base_stored")]
        s_zd, s_scat, s_xe = sem("dispatch_zeroed"), [sem("early_pairs_scattered"), sem("late_pairs_scattered")], [sem(f"xe_loaded{e}") for e in range(E)]
        s_xe0 = sem("xe_rest_loaded0")
        s_xeTp, s_xeT, s_yep = sem("xeT_psum"), sem("xeT_copied"), sem("ye_psum")
        s_z, s_nmr, s_zh, s_zg, s_zo, s_out = sem("z_step"), sem("nmr_ready"), sem("z_normed"), sem("zg_ready"), sem("out_rows_ready"), sem("out_stored")

        x_t = x.rearrange("l (j p) d -> p l j d", p=P)
        x_v = x_sb[:, :].rearrange("p (j l d) -> p l j d", l=L, d=D)
        xe_rows = xdisp.rearrange("(e s p) d -> p e s d", s=2, p=P)
        out_rows = out.rearrange("l n d -> (l n) d")

        block = ctx.enter_context(nc.Block())

        def pair(t, j):
            return t[:, bass.ds(j * PW, PW)].rearrange("p (l d) -> p l d", l=L)

        def both(t):
            return t.rearrange("p (l d) -> p l d", l=L)

        @block.sync
        def _(sp):
            sp.dma_start(w_raw[:, :, :], w_x.rearrange("(c p) d -> p c d", p=P)).then_inc(s_wx, 16)
            for l in range(L):
                sp.dma_start(x_v[:, l, 0:1, :], x_t[:, l, 0:1, :]).then_inc(s_xl0, 16)
            for l in range(L):
                sp.dma_start(x_v[:, l, 1:2, :], x_t[:, l, 1:2, :]).then_inc(s_xl1, 16)
            sp.dma_start(win_raw[:, :, :], w_in.rearrange("(c p) d -> p c d", p=P)).then_inc(s_win, 16)
            sp.dma_start(wo_raw[:, :, :], w_out.rearrange("(c p) d -> p c d", p=P)).then_inc(s_wo, 16)
            sp.dma_start(w1_sb[:, 0, :, :], w1[0].rearrange("(c p) f -> p c f", p=P)).then_inc(s_w1[0], 16)
            sp.dma_start(w2_sb[:, 0, :, :], w2[0].rearrange("(t p) d -> p t d", p=P)).then_inc(s_w2[0], 16)
            for n, v in (("bq", b_in[0:D]), ("bv", b_in[2 * D:3 * D]), ("bo", b_out), ("g1", g1), ("be1", be1), ("g2", g2), ("be2", be2)):
                sp.dma_start(rows[n][:, :], v.partition_broadcast(P)).then_inc(s_rows, 16)
            sp.wait_ge(s_zero, 2)
            sp.dma_start(b12p[0:1, :], b2.rearrange("(a e) d -> a (e d)", a=1)).then_inc(s_b2, 16)
            for l in range(L):
                sp.dma_start(x_v[:, l, 2:NJ, :], x_t[:, l, 2:NJ, :]).then_inc(s_xlr, 16)
            sp.dma_start(w1_sb[:, 1, :, :], w1[1].rearrange("(c p) f -> p c f", p=P)).then_inc(s_w1[1], 16)
            sp.dma_start(w2_sb[:, 1, :, :], w2[1].rearrange("(t p) d -> p t d", p=P)).then_inc(s_w2[1], 16)
            for e in range(E):
                sp.dma_start(xdisp[e * CAP:(e + 1) * CAP].rearrange("(p r) d -> p (r d)", p=P), zero).then_inc(s_zd, 16)
            out_t = out.rearrange("l (j p) d -> p l j d", p=P)
            with sp.Fori(1, NJ // 2) as i:
                for par in range(2):
                    e = i * 2 + par
                    sp.wait_ge(s_w12p, e - 1)
                    sp.dma_start(w1_sb[:, par, :, :], w1[bass.ds(e, 1)].rearrange("e (c p) f -> p (e c) f", p=P)).then_inc(s_w1[par], 16)
                    sp.wait_ge(s_b12, e - 1)
                    sp.dma_start(w2_sb[:, par, :, :], w2[bass.ds(e, 1)].rearrange("e (t p) d -> p (e t) d", p=P)).then_inc(s_w2[par], 16)
                    sp.wait_ge(s_based, e - 1)
                    sp.dma_start(out_t[:, :, bass.ds(e - 2, 1), :].rearrange("p l j d -> p (l j) d"), pair(base, e - 2)).then_inc(s_bst, 16)
            sp.wait_ge(s_scat[0], 16 * L * EARLY)
            sp.wait_ge(s_scat[1], 16 * L * (NJ - EARLY))
            sp.wait_ge(s_w12p, E - 1)
            sp.wait_ge(s_b12, E - 1)
            for e in range(E):
                if e == 1:
                    sp.wait_ge(s_wTp, E * 4)
                if e * 2 * DW <= WW + WW // 2 < (e + 1) * 2 * DW:
                    sp.wait_ge(s_w12p, E)
                    sp.wait_ge(s_b12, E)
                if e == 0:
                    sp.dma_start(slots[:, e, :, 0:D], xe_rows[:, e, :, 0:D]).then_inc(s_xe[e], 16)
                    sp.dma_start(slots[:, e, :, D:DW], xe_rows[:, e, :, D:DW]).then_inc(s_xe0, 16)
                else:
                    sp.dma_start(slots[:, e, :, :], xe_rows[:, e]).then_inc(s_xe[e], 16)
                if e in (2, 3):
                    j = NJ - 4 + e
                    sp.wait_ge(s_based, j + 1)
                    sp.dma_start(out_t[:, :, j], pair(base, j)).then_inc(s_bst, 16)
            sp.wait_ge(s_out, 16 * 2 * E)

        @block.gpsimd
        def _(pool):
            pool.memset(ident[:, :], 0.0).then_inc(s_ident0, 1)
            pool.wait_ge(s_ident0, 1)
            pool.affine_select(out=ident[:, :], in_=ident[:, :], compare_op=ALU.not_equal, fill=1.0, base=0,
                               pattern=[[-1, P]], channel_multiplier=1).then_inc(s_ident, 1)
            pool.dma_start(mask_i[:, :], mask.rearrange("l s -> (l s)").partition_broadcast(P)).then_inc(s_mask, 16)
            pool.dma_start(wg_sb[:, :, :], wg.rearrange("(c p) e -> p c e", p=P)).then_inc(s_mask, 16)
            pool.memset(epst[:, :], EPS).then_inc(s_const, 1)
            pool.memset(mhalf[:, :], -0.5).then_inc(s_const, 1)
            pool.wait_ge(s_const, 2)

            def rstd(n, j):
                pool.wait_ge(s_var[n], j + 1)
                if n == "z" and j:
                    pool.wait_ge(s_rs[n], j)
                var, dst = (mvz[:, j, :, 1], rsz[:, j, :]) if n == "z" else (mv[n][:, :, 1], rs[n][:, :])
                pool.tensor_tensor(ve[n][:, :], var, epst[:, :], ALU.add).then_inc(s_ve[n], 1)
                pool.wait_ge(s_ve[n], j + 1)
                pool.tensor_tensor(dst, ve[n][:, :], mhalf[:, :], ALU.pow).then_inc(s_rs[n], 1)

            def constants():
                pool.memset(b12p[:, :], 0.0).then_inc(s_zero, 1)
                pool.memset(zero, 0.0).then_inc(s_zero, 1)
                pool.memset(ones[:, :], 1.0).then_inc(s_const, 1)
                pool.memset(onesb[:, :], 1.0).then_inc(s_zw, 1)
                pool.memset(before[:, :], 1.0).then_inc(s_tri, 1)
                pool.wait_ge(s_tri, 1)
                pool.affine_select(out=before[:, :], in_=before[:, :], compare_op=ALU.is_gt, fill=0.0, base=0,
                                   pattern=[[1, P]], channel_multiplier=-1).then_inc(s_const, 1)
                for e in range(E):
                    pool.memset(rev[:, e:e + 1], float(E - e)).then_inc(s_const, 1)
                for l in range(L):
                    pool.memset(sign[:, l:l + 1], 1.0 - 2.0 * l).then_inc(s_const, 1)
                for t in range(T):
                    pool.memset(tokrow[:, t:t + 1], float(t * P - NTOK)).then_inc(s_const, 1)

            def scatter(l, j):
                pool.indirect_dma_start(out=xdisp, out_offset=bass.IndirectOffsetOnAxis(ap=slot[:, l, j:j + 1], axis=0),
                                        in_=disp[:, l * NJ + j, :], in_offset=None,
                                        bounds_check=E * CAP - 1, oob_is_err=False).then_inc(s_scat[j >= EARLY], 16)

            def without_expert(j):
                pool.wait_ge(s_zn, j - 1)
                pool.tensor_tensor(both(zw[:, :]), both(zn[:, :]), rows["g2"][:, :].unsqueeze(1).broadcast_to([P, L, D]), ALU.mult).then_inc(s_zw, 1)
                pool.wait_ge(s_zw, j)
                pool.tensor_tensor(pair(base, j - 2), both(zw[:, :]),
                                   disp_lj[:, bass.ds(j - 2, 1), :, D:2 * D].rearrange("p j l d -> p (j l) d"), ALU.add).then_inc(s_based, 1)

            def kept_rows(j, par):
                pool.wait_ge(s_xres, j * L + L)
                pool.tensor_tensor(disp_lj[:, bass.ds(j, 1), :, D:2 * D].rearrange("p j l d -> p (j l) d"), both(xres[:, :]),
                                   rows["be2"][:, :].unsqueeze(1).broadcast_to([P, L, D]), ALU.add).then_inc(s_xb, 1)
                pool.wait_ge(s_h, j + 1)
                pool.tensor_tensor(both(hb[:, par, :]), both(h_sb[:, par % 2, :]), rows["bo"][:, :].unsqueeze(1).broadcast_to([P, L, D]), ALU.add).then_inc(s_hb, 1)

            def step(j, par, cross, proj, ahead):
                if ahead:
                    rstd("x", j + 1)
                if proj:
                    rstd("y", j - 2)
                    rstd("b", j - 2)
                if cross:
                    rstd("h", j)
                    kept_rows(j, par)
                if proj:
                    without_expert(j)

            rstd("x", 0)
            constants()
            rstd("x", 1)
            rstd("h", 0)
            pool.wait_ge(s_rows, 16 * 7)
            kept_rows(0, 0)
            step(1, 1, True, False, True)
            with pool.Fori(1, NJ // 2 - 1) as i:
                for par in range(2):
                    step(i * 2 + par, par, True, True, True)
            pool.wait_ge(s_zd, 16 * E)
            step(NJ - 2, 0, True, True, True)
            step(NJ - 1, 1, True, True, False)
            pool.wait_ge(s_y1c, EARLY)
            pool.wait_ge(s_slot, L)
            for j in range(EARLY):
                scatter(0, j)
            rstd("y", NJ - 2)
            scatter(1, 0)
            scatter(1, 1)
            rstd("y", NJ - 1)
            for j in range(2, EARLY):
                scatter(1, j)
            rstd("b", NJ - 2)
            pool.wait_ge(s_scat[0], 16 * L * EARLY)
            pool.wait_ge(s_y1c, NJ)
            pool.wait_ge(s_slot, 2 * L)
            for l in range(L):
                for j in range(EARLY, NJ):
                    scatter(l, j)
            without_expert(NJ)
            rstd("b", NJ - 1)
            without_expert(NJ + 1)
            rstd("z", 0)
            rstd("z", 1)
            for e in range(E):
                if e + 2 < E:
                    rstd("z", e + 2)
                pool.wait_ge(s_zo, e + 1)
                if e == 0:
                    pool.wait_ge(s_bst, 16 * NJ)
                for s in range(2):
                    c = (e * 2 + s) * D
                    pool.indirect_dma_start(out=out_rows, out_offset=bass.IndirectOffsetOnAxis(ap=toki[:, e, s:s + 1], axis=0),
                                            in_=zo[:, c:c + D], in_offset=None,
                                            bounds_check=L * N - 1, oob_is_err=False).then_inc(s_out, 16)

        @block.scalar
        def _(act):
            act.dma_start(ctx_sb[:, :, :], ctx_in.rearrange("l s d -> s l d")).then_inc(s_ctx, 16)
            act.dma_start(diag_sb[:, :], diag.rearrange("(c p) -> c p", p=P)).then_inc(s_small, 16)
            act.dma_start(b1_sb[:, :], b1).then_inc(s_small, 16)

            def copy(dst, src, done):
                act.activation(dst, src, ACT.Copy).then_inc(done, 1)

            act.wait_ge(s_wxT, 1)
            copy(wT[:, :, :].rearrange("p c h -> p (c h)"), TB[:, :], s_setT)
            act.wait_ge(s_ctxT, 1)
            copy(ctxT[:, :, :].rearrange("p c s -> p (c s)"), WA[:, 0:DC * L * S2], s_setT)
            act.wait_ge(s_b1T, 1)
            copy(b1T[:, :, :].rearrange("p t e -> p (t e)"), AC[:, 0:FT * E], s_dn)
            act.activation(ndcol[:, :], AC[:, FT * E:FT * E + DC], ACT.Copy, scale=-1.0).then_inc(s_w12, 1)

            def winT_copy(n):
                act.wait_ge(s_winT, n + 1)
                copy(winT[:, :, n * D:(n + 1) * D], (BQ, BV, BK)[n][:, :].rearrange("p (c o) -> p c o", c=DC), (s_wT, s_setT, s_lg)[n])

            def woT_copy():
                act.wait_ge(s_woT, 1)
                copy(woT[:, :, :].rearrange("p c o -> p (c o)"), TA[:, :], s_y1T)

            def w1T_copy(j, k):
                act.wait_ge(s_wTp, j * 4 + (k + 1))
                b = (WA, WB)[k % 2]
                copy(w1T[:, 2 * k:2 * k + 2, :].rearrange("p t d -> p (t d)"), b[:, :], s_wT)

            def w12_copy(e):
                act.wait_ge(s_w12p, e + 1)
                copy(w12[:, bass.ds(e * (DC * D), DC * D)], AC[:, :], s_w12)

            def gates(n, a, b):
                act.wait_ge(s_gsh, n)
                act.activation(gex[:, :, a:b, :].rearrange("p l j e -> p l (j e)"), gsh[:, :, a:b, :].rearrange("p l j e -> p l (j e)"), ACT.Exp).then_inc(s_gex, 1)

            def hT_copy(j):
                act.wait_ge(s_hTp, j)
                copy(hT[:, :, :].rearrange("p c n -> p (c n)"), TA[:, :], s_hT)

            def oT_copy(j, b=TA):
                act.wait_ge(s_oTp, j - 1)
                copy(oT[:, :, :].rearrange("p c n -> p (c n)"), b[:, :], s_oT)

            def kvd_copy(j):
                act.wait_ge(s_kp, j)
                copy(kvd[:, :], BK[:, :], s_kvd)

            def pair_exp(j):
                act.wait_ge(s_pd, j)
                act.activation(pe2[:, :, :], dm[:, :, :], ACT.Exp, scale=HD ** -0.5).then_inc(s_pe2, 1)

            def y1_copies(j, par):
                act.wait_ge(s_y1Tp, j - 1)
                copy(y1T[:, :, :].rearrange("p c n -> p (c n)"), TA[:, :], s_y1T)
                copy(disp_lj[:, bass.ds(j - 2, 1), :, 0:D].rearrange("p j l d -> p (j l) d"), both(y1[:, par, :]), s_y1c)

            def xnT_copy(j):
                act.wait_ge(s_xnTp, j + 1)
                copy(xnT[:, :, :].rearrange("p c n -> p (c n)"), TB[:, :], s_xnT)

            def x1T_relu(j):
                act.wait_ge(s_x1p, j + 1)
                act.activation(x1T[:, :, :].rearrange("p c n -> p (c n)"), TB[:, :], ACT.Relu).then_inc(s_x1, 1)

            def scores_exp(j):
                act.wait_ge(s_shift, j + 1)
                for l in range(L):
                    last = act.activation(probs[:, l, :], shifted[:, l, :], ACT.Exp, scale=-1.0,
                                          bias=nmax[:, l:l + 1], accum_out=esum[:, l:l + 1])
                last.then_inc(s_probs, 1)

            def probsT_copy(j):
                act.wait_ge(s_prTp, j + 1)
                copy(probsT[:, :], TB[0:S2, 256:512], s_prT)

            xnT_copy(0)
            winT_copy(0)
            x1T_relu(0)
            winT_copy(1)
            winT_copy(2)
            scores_exp(0)
            w1T_copy(0, 0)
            probsT_copy(0)
            w1T_copy(0, 1)
            woT_copy()
            w1T_copy(0, 2)
            xnT_copy(1)
            w1T_copy(0, 3)
            x1T_relu(1)
            hT_copy(1)
            scores_exp(1)
            kvd_copy(1)
            probsT_copy(1)
            w12_copy(0)
            with act.Fori(1, NJ // 2) as i:
                for par in range(2):
                    j = i * 2 + par
                    w1T_copy(j - 1, 0)
                    pair_exp(j - 1)
                    w1T_copy(j - 1, 1)
                    xnT_copy(j)
                    hT_copy(j)
                    oT_copy(j)
                    x1T_relu(j)
                    kvd_copy(j)
                    w1T_copy(j - 1, 2)
                    w1T_copy(j - 1, 3)
                    scores_exp(j)
                    probsT_copy(j)
                    y1_copies(j, par)
                    w12_copy(j - 1)
            w1T_copy(E - 1, 0)
            pair_exp(NJ - 1)
            w1T_copy(E - 1, 1)
            hT_copy(NJ)
            gates(1, 0, EARLY)
            kvd_copy(NJ)
            oT_copy(NJ)
            w1T_copy(E - 1, 2)
            pair_exp(NJ)
            w1T_copy(E - 1, 3)
            oT_copy(NJ + 1, BQ)
            y1_copies(NJ, 0)
            y1_copies(NJ + 1, 1)
            gates(2, EARLY, NJ)
            w12_copy(E - 1)

            def z_norm(e):
                act.wait_ge(s_nmr, e + 1)
                for s in range(2):
                    c = (e * 2 + s) * D
                    last = act.activation(zo[:, c:c + D], zt[:, c:c + D], ACT.Identity, scale=rsz[:, e, s:s + 1], bias=nmr[:, e, s:s + 1])
                last.then_inc(s_zh, 1)

            for e in range(E + 3):
                if e < E:
                    act.wait_ge(s_xeTp, e + 1)
                    copy(xeT[:, e % 4, :, :].rearrange("p c n -> p (c n)"), xeT_banks[e % 3][:, :], s_xeT)
                if e >= 3:
                    z_norm(e - 3)

        @block.vector
        def _(dve):
            def norm_stats(n, src, j, steps, at, rstd=True):
                for l in range(L):
                    dve.bn_stats(st[n][:, l, :], src[:, l, :]).then_inc(s_ln[n], 1)
                dve.wait_ge(s_ln[n], j * steps + (at + L))
                if not isinstance(j, int):
                    dve.tensor_copy(counts[:, :], st[n][:, :, 0])
                for l in range(L):
                    last = dve.bn_aggr(mv[n][:, l, :], st[n][:, l, :])
                last.then_inc(s_var[n], 1)
                if rstd:
                    dve.wait_ge(s_rs[n], j + 1)

            def normed(n, dst, src, l):
                return dve.tensor_scalar(dst, src, mv[n][:, l, 0:1], rs[n][:, l:l + 1], ALU.subtract, ALU.mult)

            def cross_in(j):
                norm_stats("x", pair(x_sb, j), j, 2, 0)
                for l in range(L):
                    last = normed("x", xn[:, l * D:(l + 1) * D], x_sb[:, bass.ds(j * PW + l * D, D)], l)
                last.then_inc(s_xn, 1)

            def scores_shift(j):
                dve.wait_ge(s_nm, 1)
                dve.wait_ge(s_scp, j + 1)
                for l in range(L):
                    last = dve.tensor_tensor_reduce(out=shifted[:, l, :], in0=TB[:, l * S2:(l + 1) * S2], in1=nmask[:, l, :],
                                                    scale=1.0, scalar=3.0e38, op0=ALU.add, op1=ALU.min, accum_out=nmax[:, l:l + 1])
                last.then_inc(s_shift, 1)

            def cross_a(j):
                dve.wait_ge(s_probs, j + 1)
                dve.reciprocal(rsum[:, :], esum[:, :]).then_inc(s_ln["h"], 1)
                dve.wait_ge(s_attp, j + 1)
                if not isinstance(j, int) or j > 0:
                    dve.wait_ge(s_xb, j)
                dve.wait_ge(s_ln["h"], j * 3 + 1)
                for l in range(L):
                    dve.scalar_tensor_tensor(xres[:, l * D:(l + 1) * D], TB[:, l * D:(l + 1) * D], rsum[:, l:l + 1],
                                             x_sb[:, bass.ds(j * PW + l * D, D)], ALU.mult, ALU.add).then_inc(s_xres, 1)
                dve.wait_ge(s_xres, j * L + L)
                norm_stats("h", both(xres[:, :]), j, 3, 1, False)

            def cross_b(j, par):
                dve.wait_ge(s_rs["h"], j + 1)
                if not isinstance(j, int) or j > 1:
                    dve.wait_ge(s_hb, j - 1)
                for l in range(L):
                    last = normed("h", h_sb[:, par, l * D:(l + 1) * D], xres[:, l * D:(l + 1) * D], l)
                last.then_inc(s_h, 1)

            def diff(j):
                dve.wait_ge(s_hT, j)
                dve.tensor_tensor(hdT[:, :, :], hT[:, :, 0:P], hT[:, :, P:2 * P], ALU.subtract).then_inc(s_hd, 1)

            NATT = 10

            def attention_bias(j):
                dve.wait_ge(s_qp, j)
                dve.tensor_tensor(qb[:, 0:D], BQ[:, 0:D], rows["bq"][:, :], ALU.add).then_inc(s_att, 1)
                dve.tensor_tensor(qb[:, D:2 * D], BV[:, D:2 * D], rows["bq"][:, :], ALU.add).then_inc(s_att, 1)
                dve.tensor_tensor(v1b[:, :], BV[:, 0:D], rows["bv"][:, :], ALU.add).then_inc(s_qv, 1)

            def attention_a(j):
                base = (j - 1) * NATT
                dve.wait_ge(s_kvd, j)
                dve.wait_ge(s_att, base + 2)
                dve.tensor_tensor(both(prod[:, :]), both(qb[:, :]), kvd[:, 0:D].unsqueeze(1).broadcast_to([P, L, D]), ALU.mult).then_inc(s_att, 1)
                dve.wait_ge(s_att, base + 3)
                dve.tensor_reduce(dsc[:, :], prod[:, :].rearrange("p (g d) -> p g d", d=HD), AX.X, ALU.add).then_inc(s_att, 1)
                dve.wait_ge(s_att, base + 4)
                dve.tensor_scalar(dm[:, 0, :], dsc[:, :], 0.0, None, ALU.min).then_inc(s_att, 1)
                dve.tensor_scalar(dm[:, 1, :], dsc[:, :], -1.0, 0.0, ALU.mult, ALU.min).then_inc(s_pd, 1)

            def attention_b(j):
                base = (j - 1) * NATT
                dve.wait_ge(s_pe2, j)
                dve.tensor_tensor(psum2[:, :], pe2[:, 0, :], pe2[:, 1, :], ALU.add).then_inc(s_att, 1)
                dve.wait_ge(s_att, base + 6)
                dve.reciprocal(prec[:, :], psum2[:, :]).then_inc(s_att, 1)
                dve.wait_ge(s_att, base + 7)
                dve.tensor_tensor(pr[:, :], pe2[:, 0, :], prec[:, :], ALU.mult).then_inc(s_att, 1)
                dve.wait_ge(s_att, base + 8)
                for l in range(L):
                    dve.tensor_tensor(prod[:, l * D:(l + 1) * D].rearrange("p (h d) -> p h d", d=HD),
                                             kvd[:, D:2 * D].rearrange("p (h d) -> p h d", d=HD),
                                             pr[:, l * H:(l + 1) * H].unsqueeze(2).broadcast_to([P, H, HD]), ALU.mult).then_inc(s_att, 1)
                dve.wait_ge(s_att, base + 10)
                if not isinstance(j, int) or j > 1:
                    dve.wait_ge(s_oTp, j - 1)
                for l in range(L):
                    dve.tensor_tensor(o_sb[:, l * D:(l + 1) * D], prod[:, l * D:(l + 1) * D], v1b[:, :], ALU.add).then_inc(s_o, 1)

            def project_a(j, par, b=TA):
                dve.wait_ge(s_prp, j - 1)
                dve.wait_ge(s_hb, j - 1)
                dve.tensor_tensor(r_sb[:, :], b[:, :], hb[:, par, :], ALU.add).then_inc(s_r, 1)
                dve.wait_ge(s_r, j - 1)
                norm_stats("y", both(r_sb[:, :]), j - 2, 4, 0, False)

            def project_b(j, par):
                dve.wait_ge(s_var["y"], j - 1)
                for l in range(L):
                    dve.scalar_tensor_tensor(rg[:, l * D:(l + 1) * D], r_sb[:, l * D:(l + 1) * D], mv["y"][:, l, 0:1],
                                             rows["g1"][:, :], ALU.subtract, ALU.mult).then_inc(s_ln["y"], 1)
                dve.wait_ge(s_rs["y"], j - 1)
                dve.wait_ge(s_ln["y"], (j - 2) * 4 + 4)
                for l in range(L):
                    last = dve.scalar_tensor_tensor(y1[:, par, l * D:(l + 1) * D], rg[:, l * D:(l + 1) * D], rs["y"][:, l:l + 1],
                                                    rows["be1"][:, :], ALU.mult, ALU.add)
                last.then_inc(s_y1, 1)

            def base_stats(j, par):
                dve.wait_ge(s_y1, j - 1)
                norm_stats("b", both(y1[:, par, :]), j - 2, 2, 0, False)

            def base_norm(j, par):
                dve.wait_ge(s_rs["b"], j - 1)
                if not isinstance(j, int) or j > 2:
                    dve.wait_ge(s_zw, j - 1)
                for l in range(L):
                    last = normed("b", zn[:, l * D:(l + 1) * D], y1[:, par, l * D:(l + 1) * D], l)
                last.then_inc(s_zn, 1)

            def logits_copy(j):
                dve.wait_ge(s_lgp, j - 1)
                dve.tensor_copy(logits[:, :, bass.ds(j - 2, 1), :].rearrange("p l j e -> p (l j) e"),
                                BK[:, 0:L * E].rearrange("p (l e) -> p l e", l=L)).then_inc(s_lg, 1)

            def bias_sum(e, loaded, par):
                dve.wait_ge(s_w2[par], loaded)
                odd = b12p[:, bass.ds(e * D, D)]
                for k in range(FT):
                    acc = (b12t[:, :], odd)[k % 2]
                    if k == 0:
                        ins = dve.tensor_scalar(acc, w2_sb[:, par, k, :], b1T[:, k, bass.ds(e, 1)], None, ALU.mult)
                    else:
                        if k >= 2:
                            dve.wait_ge(s_bp, e * FT + (k - 1))
                        ins = dve.scalar_tensor_tensor(acc, w2_sb[:, par, k, :], b1T[:, k, bass.ds(e, 1)], acc, ALU.mult, ALU.add)
                    ins.then_inc(s_bp, 1)
                dve.wait_ge(s_bp, e * FT + FT)
                dve.tensor_tensor(odd, odd, b12t[:, :], ALU.add).then_inc(s_b12, 1)

            def step(j, loaded, par, last=False):
                diff(j)
                if not last:
                    dve.wait_ge(s_xnTp, j + 1)
                    cross_in(j + 1)
                bias_sum(j - 1, loaded, 1 - par)
                project_a(j, par)
                scores_shift(j)
                project_b(j, par)
                base_stats(j, par)
                attention_bias(j)
                cross_a(j)
                attention_a(j)
                cross_b(j, par)
                attention_b(j)
                if last:
                    diff(j + 1)
                    logits_copy(j)
                base_norm(j, par)
                if not last:
                    logits_copy(j)

            dve.wait_ge(s_xl0, 16 * L)
            cross_in(0)
            dve.wait_ge(s_mask, 32)
            dve.tensor_scalar(nmask[:, :, :].rearrange("p l s -> p (l s)"), mask_i[:, :], 1.0, NEG, ALU.subtract, ALU.mult).then_inc(s_nm, 1)
            dve.wait_ge(s_w12, 1)
            dve.wait_ge(s_x2, 1)
            for c in range(DC):
                last = dve.tensor_scalar(x2n[:, c, :], WB[:, c * L * S2:(c + 1) * L * S2], 0.0, ndcol[:, c:c + 1], ALU.max, ALU.mult)
            last.then_inc(s_x2n, 1)
            dve.wait_ge(s_xl1, 16 * L)
            dve.wait_ge(s_xnTp, 1)
            cross_in(1)
            scores_shift(0)
            cross_a(0)
            cross_b(0, 0)
            dve.wait_ge(s_dn, 1)
            dve.wait_ge(s_b2, 16)
            bias_sum(0, 16, 0)
            scores_shift(1)
            diff(1)
            dve.wait_ge(s_xlr, 16 * L)
            dve.wait_ge(s_xnTp, 2)
            cross_in(2)
            dve.wait_ge(s_rows, 16 * 7)
            attention_bias(1)
            cross_a(1)
            attention_a(1)
            cross_b(1, 1)
            attention_b(1)
            with dve.Fori(1, NJ // 2 - 1) as i:
                for par in range(2):
                    step(i * 2 + par, i * 16 + par * 16, par)
            step(NJ - 2, (NJ // 2 - 1) * 16, 0)
            step(NJ - 1, NJ // 2 * 16, 1, True)

            n = [0]

            def counted(ins):
                n[0] += 1
                ins.then_inc(s_g, 1)
                return n[0]

            def choose(k, a, b):
                lg = logits[:, :, a:b, :]
                wide = lambda t: t[:, :, a:b].unsqueeze(3).broadcast_to([P, L, b - a, E])
                revb = rev[:, :].unsqueeze(1).unsqueeze(1).broadcast_to([P, L, b - a, E])
                dve.wait_ge(s_lg, b + 1)
                largest = counted(dve.tensor_reduce(gmax[:, :, a:b], lg, AX.X, ALU.max))
                dve.wait_ge(s_g, largest)
                at_max = counted(dve.tensor_tensor(ismax[:, :, a:b, :], lg, wide(gmax), ALU.is_ge))
                dve.tensor_tensor(gsh[:, :, a:b, :], lg, wide(gmax), ALU.subtract).then_inc(s_gsh, 1)
                dve.wait_ge(s_g, at_max)
                ranked = counted(dve.tensor_tensor(rank[:, :, a:b, :], ismax[:, :, a:b, :], revb, ALU.mult))
                dve.wait_ge(s_g, ranked)
                chosen = counted(dve.tensor_reduce(first[:, :, a:b], rank[:, :, a:b, :], AX.X, ALU.max))
                dve.wait_ge(s_g, chosen)
                dve.tensor_tensor(hot[:, 0, :, a:b, :], revb, wide(first), ALU.is_equal).then_inc(s_hot, 1)

            def route(k, a, b, j=None):
                je = lambda t: t.rearrange("p l j e -> p l (j e)")
                rl = lambda t: t.rearrange("p r l j e -> p (r l) (j e)")
                places = TB[:, 0:2 * T * E].rearrange("p (r l j e) -> p r l j e", r=2, l=L, j=NJ)
                dve.wait_ge(s_hot, k)
                signed = counted(dve.tensor_tensor(je(hot[:, 1, :, a:b, :]), je(hot[:, 0, :, a:b, :]),
                                                   sign[:, :].unsqueeze(2).broadcast_to([P, L, (b - a) * E]), ALU.mult))
                if j is not None:
                    attention_bias(j)
                dve.wait_ge(s_g, signed)
                dve.wait_ge(s_pos, k)
                picked = counted(dve.tensor_tensor(rl(pick[:, :, :, a:b, :]), rl(places[:, :, :, a:b, :]), rl(hot[:, :, :, a:b, :]), ALU.mult))
                dve.wait_ge(s_gex, k)
                summed = counted(dve.tensor_reduce(gsum[:, :, a:b], gex[:, :, a:b, :], AX.X, ALU.add))
                dve.wait_ge(s_g, picked)
                located = counted(dve.tensor_reduce(loc[:, :, :, a:b].rearrange("p r l j -> p (r l) j"),
                                                    pick[:, :, :, a:b, :].rearrange("p r l j e -> p (r l) j e"), AX.X, ALU.add))
                dve.wait_ge(s_g, summed)
                counted(dve.reciprocal(disp_t[:, :, a:b, GATE], gsum[:, :, a:b]))
                if k == 1:
                    counted(dve.tensor_scalar(disp[:, :, TOK], tokrow[:, :], TB[:, 2 * T * E:2 * T * E + 1], None, ALU.add))
                dve.wait_ge(s_g, located)
                counted(dve.tensor_scalar(over[:, :, a:b], loc[:, 0, :, a:b], float(CAP), float(2 * E * CAP), ALU.is_ge, ALU.mult))
                placed = counted(dve.scalar_tensor_tensor(slotf[:, :, a:b], first[:, :, a:b], -float(CAP), loc[:, 1, :, a:b], ALU.mult, ALU.add))
                dve.wait_ge(s_g, placed)
                for l in range(L):
                    dve.scalar_tensor_tensor(slot[:, l, a:b], slotf[:, l, a:b], float(E * CAP + l * (CAP - 1)), over[:, l, a:b],
                                             ALU.add, ALU.add).then_inc(s_slot, 1)

            dve.wait_ge(s_const, 2 + 2 + E + L + T)
            choose(1, 0, EARLY)
            route(1, 0, EARLY, NJ)
            attention_a(NJ)
            attention_b(NJ)
            project_a(NJ, 0)
            project_b(NJ, 0)
            project_a(NJ + 1, 1, BQ)
            project_b(NJ + 1, 1)
            logits_copy(NJ)
            base_stats(NJ, 0)
            logits_copy(NJ + 1)
            choose(2, EARLY, NJ)
            route(2, EARLY, NJ)
            bias_sum(E - 1, NJ // 2 * 16, 1)
            base_norm(NJ, 0)
            base_stats(NJ + 1, 1)
            base_norm(NJ + 1, 1)

            def expert_sum(e):
                dve.wait_ge(s_yep, e + 1)
                for s in range(2):
                    c = (e * 2 + s) * D
                    dve.scalar_tensor_tensor(zt[:, c:c + D], ye_banks[e % len(ye_banks)][:, s * D:(s + 1) * D], slots[:, e, s, GATE:GATE + 1],
                                             slots[:, e, s, 0:D], ALU.mult, ALU.add).then_inc(s_z, 1)
                dve.tensor_scalar(toki[:, e, :], slots[:, e, :, TOK], float(NTOK), None, ALU.add).then_inc(s_z, 1)

            def sum_stats(e):
                dve.wait_ge(s_z, e * 3 + 3)
                for s in range(2):
                    c = (e * 2 + s) * D
                    dve.bn_stats(st["z"][:, s, :], zt[:, c:c + D]).then_inc(s_ln["z"], 1)

            def sum_variance(e):
                dve.wait_ge(s_ln["z"], e * 2 + 2)
                for s in range(2):
                    last = dve.bn_aggr(mvz[:, e, s, :], st["z"][:, s, :])
                last.then_inc(s_var["z"], 1)

            def minus_mean_rstd(e):
                dve.wait_ge(s_var["z"], e + 1)
                dve.wait_ge(s_rs["z"], e + 1)
                dve.scalar_tensor_tensor(nmr[:, e, :], mvz[:, e, :, 0], -1.0, rsz[:, e, :], ALU.mult, ALU.mult).then_inc(s_nmr, 1)

            def gained(e):
                zs = both(zo[:, e * 2 * D:(e + 1) * 2 * D])
                dve.wait_ge(s_zh, e + 1)
                dve.tensor_tensor(zs, zs, rows["g2"][:, :].unsqueeze(1).broadcast_to([P, 2, D]), ALU.mult).then_inc(s_zg, 1)

            def expert_out(e):
                zs = both(zo[:, e * 2 * D:(e + 1) * 2 * D])
                dve.wait_ge(s_zg, e + 1)
                dve.tensor_tensor(zs, zs, slots[:, e, :, D:2 * D], ALU.add).then_inc(s_zo, 1)

            dve.wait_ge(s_based, NJ)
            dve.wait_ge(s_xe0, 16)
            for e in range(E + 2):
                if e < E:
                    expert_sum(e)
                if e >= 2:
                    gained(e - 2)
                if 1 <= e <= E:
                    minus_mean_rstd(e - 1)
                if e < E:
                    sum_stats(e)
                if e >= 2:
                    expert_out(e - 2)
                if e < E:
                    sum_variance(e)

        @block.tensor
        def _(pe):
            places = TB[:, 0:2 * T * E].rearrange("p (r l j e) -> p r l j e", r=2, l=L, j=NJ)
            pe.wait_ge(s_ident, 1)
            pe.wait_ge(s_wx, 16)
            for c in range(DC):
                for h in range(DC):
                    last = pe.transpose(TB[:, c * D + h * P:c * D + (h + 1) * P], w_raw[:, h, c * P:(c + 1) * P], ident[:, :])
            last.then_inc(s_wxT, 1)
            pe.wait_ge(s_ctx, 16)
            for c in range(DC):
                for l in range(L):
                    last = pe.transpose(WA[:, (c * L + l) * S2:(c * L + l + 1) * S2], ctx_sb[:, l, c * P:(c + 1) * P], ident[0:S2, 0:S2])
            last.then_inc(s_ctxT, 1)
            pe.wait_ge(s_small, 32)
            pe.wait_ge(s_mask, 32)
            for t in range(FT):
                last = pe.transpose(AC[:, t * E:(t + 1) * E], b1_sb[:, t * P:(t + 1) * P], ident[0:E, 0:E])
            pe.transpose(AC[:, FT * E:FT * E + DC], diag_sb[:, :], ident[0:DC, 0:DC]).then_inc(s_b1T, 1)
            pe.wait_ge(s_setT, 2)
            for h in range(DC):
                for c in range(DC):
                    last = pe.matmul(WB[:, h * L * S2:(h + 1) * L * S2], wT[:, c, h * P:(h + 1) * P], ctxT[:, c, :], start=(c == 0), stop=(c == DC - 1))
            last.then_inc(s_x2, 1)

            def win_transposes(n, b):
                pe.wait_ge(s_win, 16)
                for c in range(DC):
                    for a in range(DC):
                        o = ((n + 1) % 3) * DC + a
                        last = pe.transpose(b[:, c * D + a * P:c * D + (a + 1) * P], win_raw[:, o, c * P:(c + 1) * P], ident[:, :])
                last.then_inc(s_winT, 1)

            def wo_transposes():
                pe.wait_ge(s_wo, 16)
                for c in range(DC):
                    for a in range(DC):
                        last = pe.transpose(TA[:, c * D + a * P:c * D + (a + 1) * P], wo_raw[:, a, c * P:(c + 1) * P], ident[:, :])
                last.then_inc(s_woT, 1)

            def w1_transpose(e, k, par):
                b = (WA, WB)[k % 2]
                pe.wait_ge(s_wT, e * 4 + (k if k >= 2 else 1))
                for a in range(2):
                    for c in range(DC):
                        last = pe.transpose(b[:, a * D + c * P:a * D + (c + 1) * P], w1_sb[:, par, c, (2 * k + a) * P:(2 * k + a + 1) * P], ident[:, :])
                last.then_inc(s_wTp, 1)

            def w12_part(c, t0, t1, par):
                for t in range(t0, t1):
                    last = pe.matmul(AC[:, c * D:(c + 1) * D], w1T[:, t, c * P:(c + 1) * P], w2_sb[:, par, t, :], start=(t == 0), stop=(t == FT - 1))
                return last

            def w12_begin(e, loaded, par):
                pe.wait_ge(s_w2[par], loaded)
                pe.wait_ge(s_w12, e + 1)
                pe.wait_ge(s_wT, e * 4 + 2)
                w12_part(0, 0, 2, par)

            def transposes(b, src):
                for c in range(DC):
                    for l in range(L):
                        last = pe.transpose(b[:, (c * L + l) * P:(c * L + l + 1) * P], src[:, l * D + c * P:l * D + (c + 1) * P], ident[:, :])
                return last

            def query_value(j):
                pe.wait_ge(s_hT, j)
                if not isinstance(j, int) or j > 1:
                    pe.wait_ge(s_qv, j - 1)
                for c in range(DC):
                    pe.matmul(BQ[:, 0:D], hT[:, c, 0:P], winT[:, c, Q * D:(Q + 1) * D], start=(c == 0), stop=(c == DC - 1))
                for c in range(DC):
                    last = pe.matmul(BV[:, :], hT[:, c, P:2 * P], winT[:, c, V * D:(Q + 1) * D], start=(c == 0), stop=(c == DC - 1))
                last.then_inc(s_qp, 1)

            def key_value_diff(j):
                pe.wait_ge(s_hd, j)
                if not isinstance(j, int) or j > 1:
                    pe.wait_ge(s_kvd, j - 1)
                    pe.wait_ge(s_lg, j - 1)
                for c in range(DC):
                    last = pe.matmul(BK[:, :], hdT[:, c, :], winT[:, c, K * D:(V + 1) * D], start=(c == 0), stop=(c == DC - 1))
                last.then_inc(s_kp, 1)

            def out_projection(j, b=TA):
                pe.wait_ge(s_oT, j - 1)
                for l in range(L):
                    for c in range(DC):
                        last = pe.matmul(b[:, l * D:(l + 1) * D], oT[:, c, l * P:(l + 1) * P], woT[:, c, :], start=(c == 0), stop=(c == DC - 1))
                last.then_inc(s_prp, 1)

            def y1_transposes(j, par):
                pe.wait_ge(s_y1, j - 1)
                transposes(TA, y1[:, par, :]).then_inc(s_y1Tp, 1)

            def router_logits(j):
                pe.wait_ge(s_y1T, j)
                for l in range(L):
                    for c in range(DC):
                        last = pe.matmul(BK[:, l * E:(l + 1) * E], y1T[:, c, l * P:(l + 1) * P], wg_sb[:, c, :], start=(c == 0), stop=(c == DC - 1))
                last.then_inc(s_lgp, 1)

            def xn_transposes(j):
                pe.wait_ge(s_xn, j + 1)
                if not isinstance(j, int) or j > 0:
                    pe.wait_ge(s_xres, j * L)
                transposes(TB, xn[:, :]).then_inc(s_xnTp, 1)

            def x1_rep(j):
                pe.wait_ge(s_xnT, j + 1)
                for h in range(DC):
                    for c in range(DC):
                        last = pe.matmul(TB[:, h * L * P:(h + 1) * L * P], wT[:, c, h * P:(h + 1) * P], xnT[:, c, :], start=(c == 0), stop=(c == DC - 1))
                last.then_inc(s_x1p, 1)

            def scores(j):
                pe.wait_ge(s_x1, j + 1)
                for l in range(L):
                    for c in range(DC):
                        last = pe.matmul(TB[:, l * S2:(l + 1) * S2], x1T[:, c, l * P:(l + 1) * P], x2n[:, c, l * S2:(l + 1) * S2], start=(c == 0), stop=(c == DC - 1))
                last.then_inc(s_scp, 1)

            def probs_transposes(j):
                pe.wait_ge(s_probs, j + 1)
                for l in range(L):
                    last = pe.transpose(TB[0:S2, 256 + l * P:256 + (l + 1) * P], probs[:, l, :], ident[:, :])
                last.then_inc(s_prTp, 1)

            def attended(j):
                pe.wait_ge(s_prT, j + 1)
                for l in range(L):
                    last = pe.matmul(TB[:, l * D:(l + 1) * D], probsT[:, l * P:(l + 1) * P], ctx_sb[:, l, :], start=True, stop=True)
                last.then_inc(s_attp, 1)

            def h_transposes(j, par):
                pe.wait_ge(s_h, j)
                if not isinstance(j, int) or j > 1:
                    pe.wait_ge(s_y1T, j - 1)
                transposes(TA, h_sb[:, 1 - par, :]).then_inc(s_hTp, 1)

            def o_transposes(j, b=TA):
                pe.wait_ge(s_o, j * L - L)
                transposes(b, o_sb[:, :]).then_inc(s_oTp, 1)

            def step(j, loaded, par):
                e = j - 1
                b = 1 - par
                pe.wait_ge(s_w1[b], loaded)
                w1_transpose(e, 0, b)
                w1_transpose(e, 1, b)
                xn_transposes(j)
                w12_begin(e, loaded, b)
                h_transposes(j, par)
                pe.wait_ge(s_wT, e * 4 + 3)
                w12_part(0, 2, 4, b)
                query_value(j)
                o_transposes(j)
                x1_rep(j)
                key_value_diff(j)
                out_projection(j)
                w1_transpose(e, 2, b)
                w1_transpose(e, 3, b)
                scores(j)
                pe.wait_ge(s_wT, e * 4 + 5)
                w12_part(0, 4, 8, b)
                probs_transposes(j)
                w12_part(1, 0, 4, b)
                attended(j)
                y1_transposes(j, par)
                w12_part(1, 4, 8, b).then_inc(s_w12p, 1)
                pe.wait_ge(s_kvd, j)
                router_logits(j)

            def count(t, l, f, b):
                pe.matmul(places[:, :, l, f:b, :], onesb[:, :], hot[:, 0, l, t, :].unsqueeze(1).unsqueeze(1).broadcast_to([P, 2, b - f, E]),
                          start=False, stop=False)

            def count_first(t, a, b, last=False):
                return pe.matmul(places[:, 0, 1, a:b, :], onesb[:, :], hot[:, 0, 0, t, :].unsqueeze(1).broadcast_to([P, b - a, E]),
                                 start=False, stop=last)

            def places_begin(k, a, b):
                if k == 1:
                    pe.wait_ge(s_xres, NJ * L)
                    pe.matmul(TB[:, 2 * T * E:2 * T * E + 1], before[:, :], onesb[:, 0:1], start=True, stop=True)
                else:
                    pe.wait_ge(s_slot, L)
                pe.matmul(places[:, :, :, a:b, :].rearrange("p r l j e -> p (r l) (j e)"), onesb[:, :],
                          before[:, 0:1].unsqueeze(1).broadcast_to([P, 2 * L, (b - a) * E]), start=True, stop=False)
                for t in range(a):
                    for l in range(L):
                        count(t, l, a, b)
                    count_first(t, a, b)

            def places_end(k, a, b):
                pe.wait_ge(s_hot, k)
                for r in range(2):
                    pe.matmul(places[:, r, :, a:b, :].rearrange("p l j e -> p l (j e)"), before[:, :],
                              hot[:, 0, :, a:b, :].rearrange("p l j e -> p l (j e)"), start=False, stop=False)
                for t in range(a, b):
                    for l in range(L):
                        if t + 1 < b:
                            count(t, l, t + 1, b)
                    last = count_first(t, a, b, t == b - 1)
                last.then_inc(s_pos, 1)

            xn_transposes(0)
            win_transposes(0, BQ)
            x1_rep(0)
            win_transposes(1, BV)
            win_transposes(2, BK)
            pe.wait_ge(s_x2n, 1)
            scores(0)
            wo_transposes()
            pe.wait_ge(s_w1[0], 16)
            w1_transpose(0, 0, 0)
            w1_transpose(0, 1, 0)
            probs_transposes(0)
            attended(0)
            w1_transpose(0, 2, 0)
            pe.wait_ge(s_dn, 1)
            w12_begin(0, 16, 0)
            xn_transposes(1)
            w1_transpose(0, 3, 0)
            pe.wait_ge(s_wT, 3)
            w12_part(0, 2, 3, 0)
            x1_rep(1)
            w12_part(0, 3, 4, 0)
            pe.wait_ge(s_y1T, 1)
            h_transposes(1, 1)
            pe.wait_ge(s_wT, 5)
            w12_part(0, 4, 6, 0)
            scores(1)
            pe.wait_ge(s_setT, 3)
            query_value(1)
            pe.wait_ge(s_lg, 1)
            key_value_diff(1)
            probs_transposes(1)
            w12_part(0, 6, 8, 0)
            attended(1)
            w12_part(1, 0, 8, 0).then_inc(s_w12p, 1)
            with pe.Fori(1, NJ // 2) as i:
                for par in range(2):
                    step(i * 2 + par, i * 16 + par * 16, par)

            pe.wait_ge(s_w1[1], NJ // 2 * 16)
            w1_transpose(E - 1, 0, 1)
            w1_transpose(E - 1, 1, 1)
            h_transposes(NJ, 0)
            w12_begin(E - 1, NJ // 2 * 16, 1)
            query_value(NJ)
            places_begin(1, 0, EARLY)
            places_end(1, 0, EARLY)
            key_value_diff(NJ)
            o_transposes(NJ)
            w1_transpose(E - 1, 2, 1)
            out_projection(NJ)
            w1_transpose(E - 1, 3, 1)

            pe.wait_ge(s_wT, (E - 1) * 4 + 3)
            w12_part(0, 2, 4, 1)
            pe.wait_ge(s_qv, NJ)
            o_transposes(NJ + 1, BQ)
            pe.wait_ge(s_wT, E * 4 + 1)
            w12_part(0, 4, 5, 1)
            out_projection(NJ + 1, BQ)
            w12_part(0, 5, 6, 1)
            y1_transposes(NJ, 0)
            w12_part(0, 6, 7, 1)
            pe.wait_ge(s_kvd, NJ)
            router_logits(NJ)
            w12_part(0, 7, 8, 1)
            w12_part(1, 0, 1, 1)
            y1_transposes(NJ + 1, 1)
            places_begin(2, EARLY, NJ)
            pe.wait_ge(s_lg, NJ)
            router_logits(NJ + 1)
            w12_part(1, 1, 3, 1)
            places_end(2, EARLY, NJ)

            def bias(e):
                pe.matmul(ye_banks[e % len(ye_banks)][:, :].rearrange("p (s d) -> p s d", s=2), ones[:, :],
                          b12p[:, e * D:(e + 1) * D].unsqueeze(1).broadcast_to([P, 2, D]), start=True, stop=False)

            def slots_transposed(e):
                pe.wait_ge(s_xe[e], 16)
                if e >= 3:
                    pe.wait_ge(s_xeT, e - 2)
                if e == 2:
                    pe.wait_ge(s_w12, E + 1)
                for c in range(DC):
                    for s in range(2):
                        last = pe.transpose(xeT_banks[e % 3][:, (c * 2 + s) * P:(c * 2 + s + 1) * P],
                                            slots[:, e, s, c * P:(c + 1) * P], ident[:, :])
                last.then_inc(s_xeTp, 1)

            pe.wait_ge(s_lg, NJ + 1)
            pe.wait_ge(s_r, NJ)
            pe.wait_ge(s_slot, 2 * L)
            w12_part(1, 3, 5, 1)
            bias(0)
            bias(1)
            pe.wait_ge(s_b12, E)
            bias(2)
            bias(3)
            pe.wait_ge(s_based, NJ - 1)
            bias(4)
            pe.wait_ge(s_scat[1], 16 * L * (NJ - EARLY))
            w12_part(1, 5, 8, 1).then_inc(s_w12p, 1)
            slots_transposed(0)
            for e in range(E):
                pe.wait_ge(s_xeT, e + 1)
                if e >= len(ye_banks):
                    pe.wait_ge(s_z, (e + 1 - len(ye_banks)) * 3)
                    bias(e)
                for s in range(2):
                    for c in range(DC):
                        last = pe.matmul(ye_banks[e % len(ye_banks)][:, s * D:(s + 1) * D], xeT[:, e % 4, c, s * P:(s + 1) * P],
                                         w12[:, (e * DC + c) * D:(e * DC + c + 1) * D], start=False, stop=(s == 1 and c == DC - 1))
                    if s == 0 and e + 1 < E:
                        slots_transposed(e + 1)
                last.then_inc(s_yep, 1)


_INS = ["x", "ctx_1024", "mask_BxS2_if1", "L0_xattn_W", "L0_xattn_diagonal", "L0_ffn_in_proj_w", "L0_ffn_in_proj_b",
        "L0_ffn_out_proj_w", "L0_ffn_out_proj_b", "L0_ffn_ln1_g", "L0_ffn_ln1_b", "L0_ffn_ln2_g", "L0_ffn_ln2_b",
        "L0_ffn_wg", "L0_ffn_w1", "L0_ffn_b1", "L0_ffn_w2", "L0_ffn_b2"]


def kernel(**inputs):
    import numpy as np
    import concourse.bacc as bacc
    from concourse.bass_utils import run_bass_kernel_spmd as run

    nc = bacc.Bacc("TRN2", target_bir_lowering=False, num_devices=1)
    arrays, args = {}, []
    for name in _INS:
        a = np.ascontiguousarray(inputs[name])
        arrays["in_" + name] = a
        args.append(nc.dram_tensor("in_" + name, a.shape, mybir.dt.from_np(a.dtype), kind="ExternalInput").ap())
    shape = inputs["x"].shape
    args.append(nc.dram_tensor("out_x", shape, F32, kind="ExternalOutput").ap())
    args.append(nc.dram_tensor("slot_rows", [shape[0] * shape[1], 2 * shape[2] + 2], F32, kind="Internal").ap())
    block_kernel(nc, *args)
    r = run(nc, [arrays], core_ids=[0])
    return r.results[0]["out_x"]
```
